# Optimizing a Trainium2 kernel written in Bass

```python
import numpy as np
import jax
import jax.numpy as jnp

def _softmax(x, axis=-1):
    return jax.nn.softmax(x, axis=axis)

def _gelu(x):
    return jax.nn.gelu(x, approximate=True)

def _silu(x):
    return jax.nn.silu(x)

def _sigmoid(x):
    return jax.nn.sigmoid(x)

def _layernorm(x, axis=-1, eps=1e-05):
    m = jnp.mean(x, axis=axis, keepdims=True)
    v = jnp.var(x, axis=axis, keepdims=True)
    return (x - m) / jnp.sqrt(v + eps)

def _scatter_add(tgt, idx, src, axis=0):
    return tgt.at[idx].add(src)

def _segment_sum(src, seg, n):
    return jax.ops.segment_sum(src, seg, n)
kernel_name = 'mk_sandwich_d1_jaxref_r4_96e569'

def setup_inputs(seed: int=0):
    np.random.seed(seed)
    _w = jnp.asarray

    def _L0_attn_setup():
        import jax, jax.numpy as jnp
        import numpy as np
        import math
        FRAME_SIZE = 144
        GAMMA = 0.5
        NUM_HEADS = 32

        def rotate_half(x):
            x1, x2 = jnp.split(x, 2, axis=-1)
            return jnp.concatenate([-x2, x1], axis=-1)

        def apply_rope(x, freqs):
            return x * jnp.cos(freqs) + rotate_half(x) * jnp.sin(freqs)

        def rope_freqs(length, dim):
            theta = 10000.0 ** (-jnp.arange(0, dim, 2, dtype=jnp.float32) / dim)
            f = jnp.arange(length, dtype=jnp.float32)[:, None] * theta[None, :]
            return jnp.concatenate([f, f], axis=-1)
        key = jax.random.key(seed)
        ks = jax.random.split(key, 9)
        B, T, C = (2, 512, 512)
        s = 0.02
        return {'hidden_states': jax.random.normal(ks[0], (B, T, C), jnp.float32), 'Wq': jax.random.normal(ks[1], (C, C), jnp.float32) * s, 'bq': jnp.zeros((C,), jnp.float32), 'Wk': jax.random.normal(ks[2], (C, C), jnp.float32) * s, 'bk': jnp.zeros((C,), jnp.float32), 'Wv': jax.random.normal(ks[3], (C, C), jnp.float32) * s, 'bv': jnp.zeros((C,), jnp.float32), 'Wo': jax.random.normal(ks[4], (C, C), jnp.float32) * s, 'bo': jnp.zeros((C,), jnp.float32)}
    _L0_attn_in = _L0_attn_setup()

    def _L0_ffn_setup():
        import jax, jax.numpy as jnp
        import numpy as np
        HIDDEN = 512
        INTER = 1408
        B, S = (2, 512)

        def _ternary(key, shape):
            return jax.random.randint(key, shape, -1, 2).astype(jnp.float32)
        key = jax.random.key(seed)
        ks = jax.random.split(key, 7)
        x = jax.random.normal(ks[0], (B, S, HIDDEN), dtype=jnp.float32)
        gate_w = _ternary(ks[1], (INTER, HIDDEN))
        up_w = _ternary(ks[2], (INTER, HIDDEN))
        down_w = _ternary(ks[3], (HIDDEN, INTER))
        gate_s = jax.random.uniform(ks[4], (INTER,), minval=0.01, maxval=0.1, dtype=jnp.float32)
        up_s = jax.random.uniform(ks[5], (INTER,), minval=0.01, maxval=0.1, dtype=jnp.float32)
        down_s = jax.random.uniform(ks[6], (HIDDEN,), minval=0.01, maxval=0.1, dtype=jnp.float32)
        return {'x': x, 'gate_w': gate_w, 'up_w': up_w, 'down_w': down_w, 'gate_s': gate_s, 'up_s': up_s, 'down_s': down_s}
    _L0_ffn_in = _L0_ffn_setup()
    _d = {'L0_attn_hidden_states': _L0_attn_in['hidden_states'], 'L0_attn_Wq': _L0_attn_in['Wq'], 'L0_attn_bq': _L0_attn_in['bq'], 'L0_attn_Wk': _L0_attn_in['Wk'], 'L0_attn_bk': _L0_attn_in['bk'], 'L0_attn_Wv': _L0_attn_in['Wv'], 'L0_attn_bv': _L0_attn_in['bv'], 'L0_attn_Wo': _L0_attn_in['Wo'], 'L0_attn_bo': _L0_attn_in['bo'], 'L0_ffn_gate_w': _L0_ffn_in['gate_w'], 'L0_ffn_up_w': _L0_ffn_in['up_w'], 'L0_ffn_down_w': _L0_ffn_in['down_w'], 'L0_ffn_gate_s': _L0_ffn_in['gate_s'], 'L0_ffn_up_s': _L0_ffn_in['up_s'], 'L0_ffn_down_s': _L0_ffn_in['down_s']}
    _x0 = _d['L0_attn_hidden_states']
    _d['L0_attn_hidden_states'] = jax.random.normal(jax.random.fold_in(jax.random.key(seed), 1), (16, 512, 512), dtype=_x0.dtype)
    del _x0
    return _d

def reference(L0_attn_hidden_states, L0_attn_Wq, L0_attn_bq, L0_attn_Wk, L0_attn_bk, L0_attn_Wv, L0_attn_bv, L0_attn_Wo, L0_attn_bo, L0_ffn_gate_w, L0_ffn_up_w, L0_ffn_down_w, L0_ffn_gate_s, L0_ffn_up_s, L0_ffn_down_s):

    def _L0_attn_ref(hidden_states, Wq, bq, Wk, bk, Wv, bv, Wo, bo):
        import jax, jax.numpy as jnp
        import numpy as np
        import math
        FRAME_SIZE = 144
        GAMMA = 0.5
        NUM_HEADS = 32

        def rotate_half(x):
            x1, x2 = jnp.split(x, 2, axis=-1)
            return jnp.concatenate([-x2, x1], axis=-1)

        def apply_rope(x, freqs):
            return x * jnp.cos(freqs) + rotate_half(x) * jnp.sin(freqs)

        def rope_freqs(length, dim):
            theta = 10000.0 ** (-jnp.arange(0, dim, 2, dtype=jnp.float32) / dim)
            f = jnp.arange(length, dtype=jnp.float32)[:, None] * theta[None, :]
            return jnp.concatenate([f, f], axis=-1)
        B, T, C = hidden_states.shape
        H = NUM_HEADS
        dh = C // H

        def split_heads(x):
            return x.reshape(B, T, H, dh).transpose(0, 2, 1, 3)
        q = split_heads(hidden_states @ Wq.T + bq)
        k = split_heads(hidden_states @ Wk.T + bk)
        v = split_heads(hidden_states @ Wv.T + bv)
        freqs_abs = rope_freqs(T, dh)[None, None]
        q = apply_rope(q, freqs_abs)
        k = apply_rope(k, freqs_abs)
        temporal_ids = jnp.floor((jnp.arange(T) // FRAME_SIZE).astype(jnp.float32) * GAMMA).astype(jnp.int32)
        n_temp = int(math.floor((T - 1) // FRAME_SIZE * GAMMA)) + 1
        freqs_temp = rope_freqs(n_temp, dh)[temporal_ids][None, None]
        q = apply_rope(q, freqs_temp)
        k = apply_rope(k, freqs_temp)
        scores = jnp.einsum('bhqd,bhkd->bhqk', q, k) / math.sqrt(dh)
        causal = jnp.tril(jnp.ones((T, T), dtype=bool))
        scores = jnp.where(causal[None, None], scores, -jnp.inf)
        weights = jax.nn.softmax(scores, axis=-1)
        out = jnp.einsum('bhqk,bhkd->bhqd', weights, v)
        out = out.transpose(0, 2, 1, 3).reshape(B, T, H * dh)
        return out @ Wo.T + bo

    def _L0_ffn_ref(x, gate_w, up_w, down_w, gate_s, up_s, down_s):
        import jax, jax.numpy as jnp
        import numpy as np
        HIDDEN = 512
        INTER = 1408
        B, S = (2, 512)

        def _ternary(key, shape):
            return jax.random.randint(key, shape, -1, 2).astype(jnp.float32)
        b, s, h = x.shape
        xf = x.reshape(b * s, h)
        g = jnp.einsum('th,ih->ti', xf, gate_w) * gate_s
        u = jnp.einsum('th,ih->ti', xf, up_w) * up_s
        hdn = jax.nn.silu(g) * u
        out = jnp.einsum('ti,hi->th', hdn, down_w) * down_s
        return out.reshape(b, s, -1)
    x = L0_attn_hidden_states
    x = x + _layernorm(_L0_attn_ref(_layernorm(x, axis=-1), L0_attn_Wq, L0_attn_bq, L0_attn_Wk, L0_attn_bk, L0_attn_Wv, L0_attn_bv, L0_attn_Wo, L0_attn_bo), axis=-1)
    x = x + _layernorm(_L0_ffn_ref(_layernorm(x, axis=-1), L0_ffn_gate_w, L0_ffn_up_w, L0_ffn_down_w, L0_ffn_gate_s, L0_ffn_up_s, L0_ffn_down_s), axis=-1)
    return x

_drawn_inputs = setup_inputs


def setup_inputs(seed=0):
    import zlib

    import numpy as np

    out = dict(_drawn_inputs(seed))
    spreads = {'L0_attn_bq': (0.0, 0.8),
     'L0_attn_bk': (0.0, 0.8),
     'L0_attn_bv': (0.0, 0.1),
     'L0_attn_bo': (0.0, 0.1)}
    factors = {}
    for name, (base, spread) in spreads.items():
        noise = np.random.default_rng([zlib.crc32(name.encode()), seed]).standard_normal(out[name].shape)
        drawn = base * np.exp(spread * noise) if base else spread * noise
        out[name] = jnp.asarray(drawn.astype(out[name].dtype))
    for name, factor in factors.items():
        out[name] = (out[name] * factor).astype(out[name].dtype)
    return out
```

```python
from contextlib import ExitStack

import numpy as np

import concourse.bass as bass
from concourse import mybir

F32 = mybir.dt.float32
F16 = mybir.dt.float16
I32 = mybir.dt.int32
ALU = mybir.AluOpType
ACT = mybir.ActivationFunctionType
AX = mybir.AxisListType
RMAX = bass.bass_isa.ReduceOp.max

P = 128
NB, T, C = 16, 512, 512
H, DH = 32, 16
NT = T // P
NC = C // P
INTER = 1408
NI = INTER // P
EPS = 1e-5
EXPONENT_BITS = 0x7F800000

HG = 4
NG = H // HG
SLOT = 64
SHIFT_UNIT = 32768.0
NU = 2 * NT


def held(engine, value):
    return value if isinstance(value, int) else engine.to_reg(value)


def wait_if_any(engine, semaphore, value):
    if not isinstance(value, int) or value > 0:
        engine.wait_ge(semaphore, value)


def power_of_two_scales(dve, pool, nc, link, largest, largest_all, power, scale, unscale, ready, reduced, waits):
    dve.wait_ge(reduced, waits)
    link(nc.vector.tensor_scalar(power, largest_all, 2.0 ** -60, 2.0 ** 60, ALU.max, ALU.min))
    link(nc.vector.tensor_scalar(power.bitcast(I32), power.bitcast(I32), EXPONENT_BITS, None, ALU.bitwise_and))
    link(nc.vector.reciprocal(scale, power))
    link(nc.vector.tensor_scalar(scale, scale, 4.0, None, ALU.mult))
    link(nc.vector.tensor_scalar(unscale, power, 0.25, None, ALU.mult))


def attention_phase(nc, x, wT, bias, rope_cos, rope_sin, x1):
    ctx = ExitStack()
    with ctx:
        def sb(name, shape, dt=F32):
            return ctx.enter_context(nc.sbuf_tensor(name, shape, dt))

        def pb(name, shape, dt=F32):
            return ctx.enter_context(nc.psum_tensor(name, shape, dt))

        def sem(name):
            return ctx.enter_context(nc.semaphore(name))

        w_hi = sb("w_hi", [P, 4, NC, C], F16)
        w_lo = sb("w_lo", [P, 4, NC, C], F16)
        bias_sb = sb("bias_sb", [P, 4, C])
        cos_sb = sb("cos_sb", [P, NT, DH])
        sin_sb = sb("sin_sb", [P, NT, DH])
        ident = sb("ident", [P, P])
        ident16 = sb("ident16", [P, P], F16)
        causal = sb("causal", [P, T])
        neg_half = sb("neg_half", [P, NT])
        largest = sb("largest", [P, 8])
        largest_all = sb("largest_all", [P, 4])
        power = sb("power", [P, 4])
        scale = sb("scale", [P, 4])
        unscale = sb("unscale", [P, 4])
        exp_scale = sb("exp_scale", [P, 1])
        out_unscale = sb("out_unscale", [P, 1])

        xn = sb("xn", [P, NT, C])
        xr = sb("xr", [P, NT, C])
        xT_hi = sb("xT_hi", [P, NC, T], F16)
        xT_lo = sb("xT_lo", [P, NC, T], F16)
        qs = sb("qs", [P, NT, H, SLOT], F16)
        ks = sb("ks", [P, NT, H, SLOT], F16)
        vs = sb("vs", [P, NT, H, 32])
        biased = sb("biased", [P, 2, C])
        turned = sb("turned", [P, 2, C])
        roped = sb("roped", [P, 2, C])
        qT = sb("qT", [P, 2, 2, T], F16)
        qmT = sb("qmT", [P, 2, 2, T], F16)
        kTz = [sb(f"kTz{j}", [P, 4, 2, T], F16) for j in range(2)]
        probs = sb("probs", [P, NT, HG, T])
        sink = sb("sink", [P, 2, T])
        row_max = sb("row_max", [P, 2, NT, HG])
        shift = sb("shift", [P, NT, HG])
        oT = sb("oT", [P, 2, T])
        recip = sb("recip", [P, NT, HG])
        attn = sb("attn", [P, NT, C])
        stats = sb("stats", [P, NT, 6])
        mv = sb("mv", [P, NT, 2])
        var = sb("var", [P, NT])
        rstd = sb("rstd", [P, NT])
        stats1 = sb("stats1", [P, NT, 6])
        mv1 = sb("mv1", [P, NT, 2])
        var1 = sb("var1", [P, NT])
        rstd1 = sb("rstd1", [P, NT])

        wide = pb("wide", [P, 4, 512])
        av = pb("av", [P, T])
        tq = pb("tq", [P, 2, T], F16)
        tk = pb("tk", [P, 2, T], F16)
        to = pb("to", [P, NT, P])

        weights_in = sem("weights_in")
        tables_in = sem("tables_in")
        consts = sem("consts")
        largest_ready = sem("largest_ready")
        largest_reduced = sem("largest_reduced")
        setup_step = sem("setup_step")
        setup_done = sem("setup_done")
        x_in = sem("x_in")
        xr_in = sem("xr_in")
        x1_out = sem("x1_out")
        var_ready = sem("var_ready")
        rstd_ready = sem("rstd_ready")
        ln1_step = sem("ln1_step")
        xn_ready = sem("xn_ready")
        wide_full = sem("wide_full")
        wide_free = sem("wide_free")
        hiT_done = sem("hiT_done")
        proj_biased = sem("proj_biased")
        turned_done = sem("turned_done")
        roped_done = sem("roped_done")
        qk_hi = sem("qk_hi")
        qk_lo = sem("qk_lo")
        tq_full = sem("tq_full")
        tq_read = sem("tq_read")
        tk_full = sem("tk_full")
        tk_read = sem("tk_read")
        s_full = sem("s_full")
        s_read = sem("s_read")
        shift_ready = sem("shift_ready")
        st_full = sem("st_full")
        st_read = sem("st_read")
        masked = sem("masked")
        av_done = sem("av_done")
        oT_ready = sem("oT_ready")
        to_full = sem("to_full")
        normed = sem("normed")
        dve_step = sem("dve_step")
        var1_ready = sem("var1_ready")
        rstd1_ready = sem("rstd1_ready")
        x1_ready = sem("x1_ready")

        N_WIDE = NC + 3 * NT + NC + NT
        F_ATT = NC + 3 * NT
        N_TQ = 2 * NG
        DVE_STEPS = 60

        tq_uses = [("q", 0), ("q", 1), ("m", 0)]
        for g in range(NG):
            tq_uses += [("q", g + 2)] if g + 2 < NG else []
            tq_uses += [("m", g + 1)] if g + 1 < NG else []

        def nth_tq(kind, g):
            return tq_uses.index((kind, g))

        block = ctx.enter_context(nc.Block())

        @block.sync
        def _(sp):
            for n in range(4):
                sp.dma_start(probs[:, n, :, :], wT[n]).then_inc(weights_in, 16)
            for n in range(4):
                sp.dma_start(bias_sb[:, n, :], bias[n]).then_inc(tables_in, 16)
            sp.dma_start(cos_sb[:, :, :], rope_cos).then_inc(tables_in, 16)
            sp.dma_start(sin_sb[:, :, :], rope_sin).then_inc(tables_in, 16)
            sp.dma_start(xn[:, :, :], x[0, :, :, :]).then_inc(x_in, 16)

            def sequence(i, last):
                sp.wait_ge(x1_out, 16 * i)
                sp.dma_start(xr[:, :, :], x[i, :, :, :]).then_inc(xr_in, 16)
                if not last:
                    sp.wait_ge(wide_full, N_WIDE * i + NC)
                    sp.dma_start(xn[:, :, :], x[i + 1, :, :, :]).then_inc(x_in, 16)
                sp.wait_ge(x1_ready, i + 1)
                sp.dma_start(x1[i, :, :, :], xr[:, :, :]).then_inc(x1_out, 16)

            with sp.Fori(0, NB - 1) as i:
                sequence(i, False)
            sequence(NB - 1, True)
            sp.wait_ge(x1_out, 16 * NB)

        @block.gpsimd
        def _(pool):
            nc.gpsimd.memset(ident[:, :], 0.0).then_inc(consts, 1)
            nc.gpsimd.memset(ident16[:, :], 0.0).then_inc(consts, 1)
            nc.gpsimd.memset(causal[:, :], 0.0).then_inc(consts, 1)
            nc.gpsimd.memset(neg_half[:, :], -0.5).then_inc(consts, 1)
            pool.wait_ge(consts, 4)
            for m in (ident, ident16):
                nc.gpsimd.affine_select(out=m[:, :], in_=m[:, :], compare_op=ALU.not_equal, fill=1.0, base=0,
                                        pattern=[[-1, P]], channel_multiplier=1).then_inc(consts, 1)
            tri = causal[:, T - P:T]
            nc.gpsimd.affine_select(out=tri, in_=tri, compare_op=ALU.is_ge, fill=-1e38, base=0,
                                    pattern=[[-1, P]], channel_multiplier=1).then_inc(consts, 1)
            pool.wait_ge(largest_ready, 1)
            nc.gpsimd.partition_all_reduce(largest_all[:, :], largest[:, 0:4], P, RMAX).then_inc(largest_reduced, 1)

            def inverse_root(i, ready, v, out, done):
                pool.wait_ge(ready, i + 1)
                nc.gpsimd.tensor_tensor(out, v, neg_half[:, :], ALU.pow).then_inc(done, 1)

            inverse_root(0, var_ready, var[:, :], rstd[:, :], rstd_ready)

            def sequence(i, last):
                for n in range(2 * NT):
                    t = n % NT
                    pool.wait_ge(proj_biased, 2 * NT * i + n + 1)
                    a = biased[:, n % 2, :].rearrange("p (h d) -> p h d", h=H)
                    o = turned[:, n % 2, :].rearrange("p (h d) -> p h d", h=H)
                    s = sin_sb[:, t:t + 1, :]
                    half = DH // 2
                    nc.gpsimd.tensor_tensor(o[:, :, 0:half], a[:, :, half:DH],
                                            s[:, :, 0:half].broadcast_to([P, H, half]), ALU.mult)
                    nc.gpsimd.tensor_tensor(o[:, :, half:DH], a[:, :, 0:half],
                                            s[:, :, half:DH].broadcast_to([P, H, half]),
                                            ALU.mult).then_inc(turned_done, 1)
                for n in range(NG * NT):
                    kt = n % NT
                    exps_done = held(pool, NG * NU * i + 2 * n + 2)
                    pool.wait_ge(consts, 7)
                    pool.wait_ge(st_read, exps_done)
                    d = probs[:, kt, :, P * kt:P * kt + P]
                    nc.gpsimd.affine_select(out=d, in_=d, compare_op=ALU.is_ge, fill=0.0, base=0,
                                            pattern=[[0, HG], [1, P]], channel_multiplier=-1).then_inc(masked, 1)
                if not last:
                    inverse_root(i + 1, var_ready, var[:, :], rstd[:, :], rstd_ready)
                inverse_root(i, var1_ready, var1[:, :], rstd1[:, :], rstd1_ready)

            with pool.Fori(0, NB - 1) as i:
                sequence(i, False)
            sequence(NB - 1, True)

        @block.scalar
        def _(act):
            def sequence(i):
                def transposed_hi(c, use):
                    act.wait_ge(wide_full, N_WIDE * i + use + 1)
                    nc.scalar.activation(xT_hi[:, c, :], wide[:, use % 4, :], ACT.Copy).then_inc(hiT_done, 1)

                def read_q(kind, g):
                    act.wait_ge(tq_full, N_TQ * i + nth_tq(kind, g) + 1)
                    dst = qT if kind == "q" else qmT
                    nc.scalar.activation(dst[:, g % 2, :, :], tq[:, :, :], ACT.Copy).then_inc(tq_read, 1)

                def read_k(g):
                    act.wait_ge(tk_full, NG * i + g + 1)
                    nc.scalar.activation(kTz[0][0:SLOT, g % 4, :, :], tk[0:SLOT, :, :], ACT.Copy)
                    nc.scalar.activation(kTz[1][SLOT:P, g % 4, :, :], tk[SLOT:P, :, :], ACT.Copy).then_inc(tk_read, 1)

                for c in range(NC):
                    transposed_hi(c, c)
                for n in range(2 * NT):
                    t = n % NT
                    act.wait_ge(roped_done, 2 * NT * i + n + 1)
                    src = roped[:, n % 2, :].rearrange("p (h o d) -> p h o d", h=H, o=1).broadcast_to([P, H, 2, DH])
                    dst = (ks if n < NT else qs)[:, t, :, :].rearrange("p h (s d) -> p h s d", d=DH)
                    dst = dst[:, :, 0:2, :] if n < NT else dst[:, :, 0:3:2, :]
                    nc.scalar.activation(dst, src, ACT.Copy).then_inc(qk_hi, 1)
                read_q("q", 0)
                read_k(0)
                read_q("q", 1)
                read_k(1)
                read_q("m", 0)
                for g in range(NG):
                    for u in range(NU):
                        kt, pair = divmod(u, 2)
                        if g > 0:
                            act.wait_ge(av_done, NG * NT * i + NT * (g - 1) + kt + 1)
                        act.wait_ge(st_full, NG * NU * i + NU * g + u + 1)
                        nc.scalar.activation(probs[:, kt, 2 * pair:2 * pair + 2, P * kt:T], wide[:, 0:2, 0:T - P * kt],
                                             ACT.Exp, scale=exp_scale[:, 0:1]).then_inc(st_read, 1)
                        if u == 1 and g > 0:
                            read_o(i, g - 1)
                        if u == 4 and g + 2 < NG:
                            read_q("q", g + 2)
                            read_k(g + 2)
                    if g + 1 < NG:
                        read_q("m", g + 1)
                read_o(i, NG - 1)
                for c in range(NC):
                    transposed_hi(c, F_ATT + c)

            def read_o(i, g):
                act.wait_ge(av_done, NG * NT * i + NT * (g + 1))
                act.wait_ge(to_full, NG * i + max(g - 1, 0))
                nc.scalar.activation(oT[:, g % 2, :], av[:, :], ACT.Copy).then_inc(oT_ready, 1)

            act.wait_ge(setup_done, 1)
            with act.Fori(0, NB) as i:
                sequence(i)

        @block.vector
        def _(dve):
            steps = [0]

            def setup(ins):
                steps[0] += 1
                ins.then_inc(setup_step, 1)
                dve.wait_ge(setup_step, steps[0])

            nc.vector.memset(qs[:, :, :, :], 0.0)
            nc.vector.memset(ks[:, :, :, :], 0.0)
            nc.vector.memset(vs[:, :, :, :], 0.0)
            nc.vector.memset(kTz[0][:, :, :, :], 0.0)
            setup(nc.vector.memset(kTz[1][:, :, :, :], 0.0))
            nc.vector.memset(ks[:, :, :, 3 * DH:3 * DH + 2], SHIFT_UNIT)
            setup(nc.vector.memset(vs[:, :, :, DH:DH + 1], 1.0))
            dve.wait_ge(weights_in, 64)
            dve.wait_ge(tables_in, 96)
            for n in range(4):
                nc.vector.tensor_reduce(largest[:, n:n + 1], probs[:, n, :, :], AX.XY, ALU.max,
                                        apply_absolute_value=True)
                last = nc.vector.tensor_reduce(largest[:, 4 + n:5 + n], bias_sb[:, n, :], AX.X, ALU.max,
                                               apply_absolute_value=True)
            setup(last)
            setup(nc.vector.tensor_scalar(largest[:, 4:8], largest[:, 4:8], 1.0 / C, None, ALU.mult))
            nc.vector.tensor_tensor(largest[:, 0:4], largest[:, 0:4], largest[:, 4:8], ALU.max).then_inc(largest_ready, 1)
            power_of_two_scales(dve, None, nc, setup, largest, largest_all[:, :], power[:, :], scale[:, :],
                                unscale[:, :], largest_ready, largest_reduced, 1)
            for n in range(3):
                nc.vector.tensor_scalar(bias_sb[:, n, :], bias_sb[:, n, :], scale[:, n:n + 1], None, ALU.mult)
            nc.vector.tensor_scalar(exp_scale[:, :], unscale[:, 0:1], unscale[:, 1:2], DH ** -0.5, ALU.mult, ALU.mult)
            nc.vector.tensor_scalar(out_unscale[:, :], unscale[:, 2:3], unscale[:, 3:4], None, ALU.mult)
            for n in range(4):
                last = nc.vector.tensor_scalar(w_hi[:, n, :, :], probs[:, n, :, :], scale[:, n:n + 1], None, ALU.mult)
            setup(last)
            for n in range(4):
                last = nc.vector.scalar_tensor_tensor(w_lo[:, n, :, :], probs[:, n, :, :], scale[:, n:n + 1],
                                                      w_hi[:, n, :, :], ALU.mult, ALU.subtract)
            last.then_inc(setup_done, 1)
            dve.wait_ge(setup_done, 1)
            dve.wait_ge(consts, 7)

            def ln1(i, k):
                def step(ins, stats_next=False):
                    step.n += 1
                    ins.then_inc(ln1_step, 1)
                    done = held(dve, 2 * k + step.n)
                    if stats_next:
                        dve.wait_ge(setup_done, 1)
                    dve.wait_ge(ln1_step, done)
                step.n = 0
                dve.wait_ge(x_in, 16 * k + 16)
                for t in range(NT):
                    last = nc.vector.bn_stats(stats[:, t, :], xn[:, t, :])
                step(last, True)
                for t in range(NT):
                    last = nc.vector.bn_aggr(mv[:, t, :], stats[:, t, :])
                step(last)
                nc.vector.tensor_scalar(var[:, :], mv[:, :, 1], EPS, None, ALU.add).then_inc(var_ready, 1)
                dve.wait_ge(rstd_ready, k + 1)
                for t in range(NT):
                    last = nc.vector.tensor_scalar(xn[:, t, :], xn[:, t, :], mv[:, t, 0:1], rstd[:, t:t + 1],
                                                   ALU.subtract, ALU.mult)
                last.then_inc(xn_ready, 1)

            def sequence(i, last_sequence):
                taken = [0]

                def step(ins, stats_next=False):
                    taken[0] += 1
                    ins.then_inc(dve_step, 1)
                    done = held(dve, DVE_STEPS * i + taken[0])
                    if stats_next:
                        dve.wait_ge(setup_done, 1)
                    dve.wait_ge(dve_step, done)

                def transposed_lo(c, use):
                    dve.wait_ge(hiT_done, 2 * NC * i + c + 1 + (NC if use >= F_ATT else 0))
                    nc.vector.tensor_tensor(xT_lo[:, c, :], wide[:, use % 4, :], xT_hi[:, c, :],
                                            ALU.subtract).then_inc(wide_free, 1)

                for c in range(NC):
                    transposed_lo(c, c)

                def project(n):
                    dve.wait_ge(wide_full, N_WIDE * i + NC + n + 1)
                    if n < 2 * NT:
                        t, which = n % NT, 1 - n // NT
                        dve.wait_ge(turned_done, 2 * NT * i + max(n - 1, 0))
                        nc.vector.tensor_tensor(biased[:, n % 2, :], wide[:, (NC + n) % 4, :], bias_sb[:, which, :],
                                                ALU.add).then_inc(wide_free, 1)
                        dve.wait_ge(wide_free, N_WIDE * i + NC + n + 1)
                        dve.wait_ge(qk_hi, 2 * NT * i + max(n - 1, 0))
                        r = roped[:, n % 2, :].rearrange("p (h d) -> p h d", h=H)
                        nc.vector.tensor_tensor(r, biased[:, n % 2, :].rearrange("p (h d) -> p h d", h=H),
                                                cos_sb[:, t:t + 1, :].broadcast_to([P, H, DH]),
                                                ALU.mult).then_inc(proj_biased, 1)
                    else:
                        t = n - 2 * NT
                        nc.vector.tensor_tensor(vs[:, t, :, 0:DH],
                                                wide[:, (NC + n) % 4, :].rearrange("p (h d) -> p h d", h=H),
                                                bias_sb[:, 2, :].rearrange("p (h d) -> p h d", h=H),
                                                ALU.add).then_inc(wide_free, 1)

                def rotate(n):
                    dve.wait_ge(turned_done, 2 * NT * i + n + 1)
                    nc.vector.tensor_tensor(roped[:, n % 2, :], roped[:, n % 2, :], turned[:, n % 2, :],
                                            ALU.add).then_inc(roped_done, 1)

                def low(n):
                    t = n % NT
                    dst, at = (ks, 2 * DH) if n < NT else (qs, DH)
                    dve.wait_ge(qk_hi, 2 * NT * i + n + 1)
                    nc.vector.tensor_tensor(dst[:, t, :, at:at + DH],
                                            roped[:, n % 2, :].rearrange("p (h d) -> p h d", h=H),
                                            dst[:, t, :, 0:DH], ALU.subtract).then_inc(qk_lo, 1)

                for n in range(3 * NT):
                    if 2 <= n and n - 2 < 2 * NT:
                        low(n - 2)
                        if n == 2:
                            nc.vector.memset(qs[:, :, :, 3 * DH:3 * DH + 2], 0.0)
                    project(n)
                    if 1 <= n and n - 1 < 2 * NT:
                        rotate(n - 1)

                def norm(g):
                    dve.wait_ge(to_full, NG * i + g + 1)
                    o = to[:, :, :].rearrange("p t (h c) -> p t h c", c=32)
                    step(nc.vector.reciprocal(recip[:, :, :], o[:, :, :, DH]))
                    r = recip[:, :, :].rearrange("p t (h o) -> p t h o", o=1).broadcast_to([P, NT, HG, DH])
                    dst = attn[:, :, HG * DH * g:HG * DH * (g + 1)].rearrange("p t (h d) -> p t h d", h=HG)
                    nc.vector.tensor_tensor(dst, o[:, :, :, 0:DH], r, ALU.mult).then_inc(normed, 1)

                for s in range(NG * NU):
                    g, u = divmod(s, NU)
                    qt, pair = divmod(u, 2)
                    n = P * (qt + 1)
                    for j in range(2):
                        h = 2 * s + j
                        sink_written = held(dve, 2 * NG * NU * i + max(h - 1, 0))
                        filled = held(dve, 2 * NG * NU * i + h + 1)
                        dve.wait_ge(consts, 7)
                        dve.wait_ge(s_read, sink_written)
                        dve.wait_ge(s_full, filled)
                        nc.vector.tensor_tensor_reduce(
                            out=sink[:, h % 2, 0:n], in0=wide[:, 2 + h % 2, 0:n], in1=causal[:, T - n:T], scale=1.0,
                            scalar=-3e38, op0=ALU.add, op1=ALU.max,
                            accum_out=row_max[:, g % 2, qt, 2 * pair + j:2 * pair + j + 1]).then_inc(s_read, 1)
                    if u == NU - 1:
                        dve.wait_ge(s_read, 2 * NG * NU * i + 2 * (s + 1))
                        step(nc.vector.tensor_scalar(shift[:, :, :], row_max[:, g % 2, :, :], -1.0 / SHIFT_UNIT, None,
                                                     ALU.mult))
                        m = qs[:, :, HG * g:HG * (g + 1), :]
                        step(nc.vector.tensor_copy(m[:, :, :, 3 * DH], shift[:, :, :]))
                        nc.vector.tensor_tensor(m[:, :, :, 3 * DH + 1], shift[:, :, :], m[:, :, :, 3 * DH],
                                                ALU.subtract).then_inc(shift_ready, 1)
                    if u == 5 and g >= 2:
                        norm(g - 2)
                if not last_sequence:
                    ln1(i, i + 1)
                norm(NG - 2)
                norm(NG - 1)
                for c in range(NC):
                    transposed_lo(c, F_ATT + c)

                for t in range(NT):
                    use = F_ATT + NC + t
                    dve.wait_ge(wide_full, N_WIDE * i + use + 1)
                    nc.vector.scalar_tensor_tensor(attn[:, t, :], wide[:, use % 4, :], out_unscale[:, 0:1],
                                                   bias_sb[:, 3, :], ALU.mult, ALU.add).then_inc(wide_free, 1)
                    dve.wait_ge(wide_free, N_WIDE * i + use + 1)
                    last = nc.vector.bn_stats(stats1[:, t, :], attn[:, t, :])
                step(last, True)
                for t in range(NT):
                    last = nc.vector.bn_aggr(mv1[:, t, :], stats1[:, t, :])
                step(last)
                nc.vector.tensor_scalar(var1[:, :], mv1[:, :, 1], EPS, None, ALU.add).then_inc(var1_ready, 1)
                dve.wait_ge(rstd1_ready, i + 1)
                for t in range(NT):
                    last = nc.vector.tensor_scalar(attn[:, t, :], attn[:, t, :], mv1[:, t, 0:1], rstd1[:, t:t + 1],
                                                   ALU.subtract, ALU.mult)
                step(last)
                dve.wait_ge(xr_in, 16 * i + 16)
                nc.vector.tensor_tensor(xr[:, :, :], xr[:, :, :], attn[:, :, :], ALU.add).then_inc(x1_ready, 1)
                while taken[0] < DVE_STEPS:
                    step(nc.vector.memset(shift[:, 0, 0:1], 0.0))
                assert taken[0] == DVE_STEPS

            ln1(0, 0)
            with dve.Fori(0, NB - 1) as i:
                sequence(i, False)
            sequence(NB - 1, True)

        @block.tensor
        def _(pe):
            def sequence(i):
                def free(use):
                    pe.wait_ge(wide_free, N_WIDE * i + max(use - 3, 0))

                def three_products(out, a_hi, a_lo, b_hi, b_lo, first, last):
                    nc.tensor.matmul(out, a_hi, b_hi, start=first, stop=False)
                    nc.tensor.matmul(out, a_hi, b_lo, start=False, stop=False)
                    return nc.tensor.matmul(out, a_lo, b_hi, start=False, stop=last)

                def transpose_in(src, c, use):
                    for t in range(NT):
                        last = nc.tensor.transpose(wide[:, use % 4, P * t:P * (t + 1)], src[:, t, P * c:P * (c + 1)],
                                                   ident[:, :])
                    last.then_inc(wide_full, 1)

                def project(w, t, use):
                    for c in range(NC):
                        last = three_products(wide[:, use % 4, :], xT_hi[:, c, P * t:P * (t + 1)],
                                              xT_lo[:, c, P * t:P * (t + 1)], w_hi[:, w, c, :], w_lo[:, w, c, :],
                                              c == 0, c == NC - 1)
                    last.then_inc(wide_full, 1)

                def transpose_q(kind, g):
                    use = nth_tq(kind, g)
                    pe.wait_ge(tq_read, N_TQ * i + use)
                    for pair in range(2):
                        for t in range(NT):
                            h = HG * g + 2 * pair
                            last = nc.tensor.transpose(tq[:, pair, P * t:P * (t + 1)],
                                                       qs[:, t, h:h + 2, :].rearrange("p h s -> p (h s)"), ident16[:, :])
                    last.then_inc(tq_full, 1)

                def transpose_k(g):
                    pe.wait_ge(tk_read, NG * i + g)
                    for pair in range(2):
                        for t in range(NT):
                            h = HG * g + 2 * pair
                            last = nc.tensor.transpose(tk[:, pair, P * t:P * (t + 1)],
                                                       ks[:, t, h:h + 2, :].rearrange("p h s -> p (h s)"), ident16[:, :])
                    last.then_inc(tk_full, 1)

                def score(s, j):
                    g, u = divmod(s, NU)
                    qt, pair = divmod(u, 2)
                    h = 2 * s + j
                    if u == 0 and j == 0:
                        pe.wait_ge(tq_read, N_TQ * i + nth_tq("q", g) + 1)
                        pe.wait_ge(tk_read, NG * i + g + 1)
                    if h < 2:
                        pe.wait_ge(wide_free, N_WIDE * i + F_ATT)
                    else:
                        pe.wait_ge(s_read, 2 * NG * NU * i + h - 1)
                    nc.tensor.matmul(wide[:, 2 + h % 2, 0:P * (qt + 1)], qT[:, g % 2, pair, P * qt:P * (qt + 1)],
                                     kTz[j][:, g % 4, pair, 0:P * (qt + 1)], start=True, stop=True).then_inc(s_full, 1)

                def score_transposed(g, u):
                    kt, pair = divmod(u, 2)
                    n = NU * g + u
                    if u == 0:
                        pe.wait_ge(tq_read, N_TQ * i + nth_tq("m", g) + 1)
                    if n == 0:
                        pe.wait_ge(wide_free, N_WIDE * i + F_ATT)
                    else:
                        pe.wait_ge(st_read, NG * NU * i + n)
                    for j in range(2):
                        last = nc.tensor.matmul(wide[:, j, 0:T - P * kt], kTz[j][:, g % 4, pair, P * kt:P * (kt + 1)],
                                                qmT[:, g % 2, pair, P * kt:T], start=True, stop=True)
                    last.then_inc(st_full, 1)

                def weigh(g, kt):
                    pe.wait_ge(masked, NG * NT * i + NT * g + kt + 1)
                    if kt == 0:
                        pe.wait_ge(oT_ready, NG * i + g)
                    for j in range(HG):
                        last = nc.tensor.matmul(av[32 * j:32 * j + 32, P * kt:T], vs[:, kt, HG * g + j, :],
                                                probs[:, kt, j, P * kt:T], start=kt == 0, stop=kt == NT - 1,
                                                tile_position=(0, 32 * j), skip_group_check=True)
                    last.then_inc(av_done, 1)

                def transpose_o(g):
                    pe.wait_ge(oT_ready, NG * i + g + 1)
                    pe.wait_ge(normed, NG * i + g)
                    for t in range(NT):
                        last = nc.tensor.transpose(to[:, t, :], oT[:, g % 2, P * t:P * (t + 1)], ident[:, :])
                    last.then_inc(to_full, 1)

                pe.wait_ge(xn_ready, i + 1)
                for c in range(NC):
                    free(c)
                    transpose_in(xn, c, c)
                for n in range(3 * NT):
                    use = NC + n
                    free(max(use, 2 * NC - 1) if n == 0 else use)
                    project((1, 0, 2)[n // NT], n % NT, use)
                pe.wait_ge(qk_lo, 2 * NT * (i + 1))
                for g in range(2):
                    transpose_q("q", g)
                    transpose_k(g)
                for s in range(NU + 2):
                    score(s, 0)
                    score(s, 1)
                pe.wait_ge(shift_ready, NG * i + 1)
                transpose_q("m", 0)
                for g in range(NG):
                    for u in range(NU):
                        s = NU * (g + 1) + u + 2
                        if s < NG * NU:
                            score(s, 0)
                        score_transposed(g, u)
                        if s < NG * NU:
                            score(s, 1)
                        if u == 1 and g > 0:
                            transpose_o(g - 1)
                        if u in (3, 5, 7):
                            weigh(g, (u - 3) // 2)
                        if u == 3 and g + 2 < NG:
                            transpose_q("q", g + 2)
                            transpose_k(g + 2)
                    if g + 1 < NG:
                        pe.wait_ge(shift_ready, NG * i + g + 2)
                        transpose_q("m", g + 1)
                    weigh(g, NT - 1)
                transpose_o(NG - 1)
                pe.wait_ge(normed, NG * (i + 1))
                pe.wait_ge(st_read, NG * NU * (i + 1))
                pe.wait_ge(s_read, 2 * NG * NU * (i + 1))
                for c in range(NC):
                    transpose_in(attn, c, F_ATT + c)
                pe.wait_ge(wide_free, N_WIDE * i + F_ATT + NC)
                for t in range(NT):
                    project(3, t, F_ATT + NC + t)

            pe.wait_ge(setup_done, 1)
            pe.wait_ge(consts, 7)
            with pe.Fori(0, NB) as i:
                sequence(i)


def ffn_phase(nc, x1, gateT, upT, downT, gate_s, up_s, down_s, out):
    ctx = ExitStack()
    with ctx:
        def sb(name, shape, dt=F32):
            return ctx.enter_context(nc.sbuf_tensor(name, shape, dt))

        def pb(name, shape, dt=F32):
            return ctx.enter_context(nc.psum_tensor(name, shape, dt))

        def sem(name):
            return ctx.enter_context(nc.semaphore(name))

        raw = [sb("raw_gate", [P, NC, INTER]), sb("raw_up", [P, NC, INTER]), sb("raw_down", [P, NI, C])]
        gate_hi = sb("gate_hi", [P, NC, INTER], F16)
        gate_lo = sb("gate_lo", [P, NC, INTER], F16)
        up_hi = sb("up_hi", [P, NC, INTER], F16)
        up_lo = sb("up_lo", [P, NC, INTER], F16)
        down_hi = sb("down_hi", [P, NI, C], F16)
        down_lo = sb("down_lo", [P, NI, C], F16)
        ident = sb("f_ident", [P, P])
        neg_half = sb("f_neg_half", [P, NT])
        scales = sb("scales", [P, 3, NI])
        down_row = sb("down_row", [P, C])
        largest = sb("f_largest", [P, 6])
        largest_all = sb("f_largest_all", [P, 6])
        power = sb("f_power", [P, 4])
        scale = sb("f_scale", [P, 4])
        unscale = sb("f_unscale", [P, 4])
        gate_scale = sb("gate_scale", [P, NI])
        up_scale = sb("up_scale", [P, NI])
        rest = sb("rest", [P, 4])
        rest_all = sb("rest_all", [P, 1])
        has_rest = sb("has_rest", [P, 1])

        xn = sb("f_xn", [P, NT, C])
        xr = sb("f_xr", [P, NT, C])
        xT_hi = sb("f_xT_hi", [P, NC, T], F16)
        xT_lo = sb("f_xT_lo", [P, NC, T], F16)
        silu = sb("silu", [P, 2, T])
        hidden = sb("hidden", [P, 2, T])
        hid_hi = sb("hid_hi", [P, 3, T], F16)
        hid_lo = sb("hid_lo", [P, 3, T], F16)
        y = sb("y", [P, NT, C])
        stats = sb("f_stats", [P, NT, 6])
        mv = sb("f_mv", [P, NT, 2])
        var = sb("f_var", [P, NT])
        rstd = sb("f_rstd", [P, NT])
        stats1 = sb("f_stats1", [P, NT, 6])
        mv1 = sb("f_mv1", [P, NT, 2])
        var1 = sb("f_var1", [P, NT])
        rstd1 = sb("f_rstd1", [P, NT])

        gu = pb("gu", [P, 4, 512])
        down = pb("down", [P, NT, 512])

        weights_in = sem("f_weights_in")
        tables_in = sem("f_tables_in")
        consts = sem("f_consts")
        largest_ready = sem("f_largest_ready")
        largest_reduced = sem("f_largest_reduced")
        setup_step = sem("f_setup_step")
        setup_done = sem("f_setup_done")
        x_in = sem("f_x_in")
        xr_in = sem("f_xr_in")
        out_done = sem("out_done")
        var_ready = sem("f_var_ready")
        rstd_ready = sem("f_rstd_ready")
        ln_step = sem("ln_step")
        xn_ready = sem("f_xn_ready")
        xT_full = sem("xT_full")
        hiT_done = sem("f_hiT_done")
        loT_done = sem("loT_done")
        gate_full = sem("gate_full")
        up_full = sem("up_full")
        silu_done = sem("silu_done")
        hidden_done = sem("hidden_done")
        hid_hi_done = sem("hid_hi_done")
        hid_lo_done = sem("hid_lo_done")
        down_step = sem("down_step")
        down_read = sem("down_read")
        var1_ready = sem("f_var1_ready")
        rstd1_ready = sem("f_rstd1_ready")
        end_step = sem("end_step")
        out_ready = sem("out_ready")

        block = ctx.enter_context(nc.Block())

        @block.sync
        def _(sp):
            for r, w in zip(raw, (gateT, upT, downT)):
                sp.dma_start(r[:, :, :], w).then_inc(weights_in, 16)
            sp.dma_start(scales[:, 0, :], gate_s).then_inc(tables_in, 16)
            sp.dma_start(scales[:, 1, :], up_s).then_inc(tables_in, 16)
            sp.dma_start(down_row[:, :], down_s).then_inc(tables_in, 16)
            sp.dma_start(xn[:, :, :], x1[0, :, :, :]).then_inc(x_in, 16)

            def sequence(i, last):
                wait_if_any(sp, out_ready, i)
                if not isinstance(i, int) or i > 0:
                    sp.dma_start(out[i - 1, :, :, :], xr[:, :, :]).then_inc(out_done, 16)
                wait_if_any(sp, out_done, 16 * i)
                sp.dma_start(xr[:, :, :], x1[i, :, :, :]).then_inc(xr_in, 16)
                if not last:
                    sp.wait_ge(xT_full, NC * (i + 1))
                    sp.dma_start(xn[:, :, :], x1[i + 1, :, :, :]).then_inc(x_in, 16)

            sequence(0, False)
            with sp.Fori(1, NB - 1) as i:
                sequence(i, False)
            sequence(NB - 1, True)
            sp.wait_ge(out_ready, NB)
            sp.dma_start(out[NB - 1, :, :, :], xr[:, :, :]).then_inc(out_done, 16)
            sp.wait_ge(out_done, 16 * NB)

        @block.gpsimd
        def _(pool):
            nc.gpsimd.memset(ident[:, :], 0.0).then_inc(consts, 1)
            nc.gpsimd.memset(neg_half[:, :], -0.5).then_inc(consts, 1)
            pool.wait_ge(consts, 2)
            nc.gpsimd.affine_select(out=ident[:, :], in_=ident[:, :], compare_op=ALU.not_equal, fill=1.0, base=0,
                                    pattern=[[-1, P]], channel_multiplier=1).then_inc(consts, 1)
            pool.wait_ge(largest_ready, 1)
            nc.gpsimd.partition_all_reduce(largest_all[:, 0:5], largest[:, 0:5], P, RMAX).then_inc(largest_reduced, 1)
            pool.wait_ge(largest_ready, 2)
            nc.gpsimd.partition_all_reduce(rest_all[:, :], rest[:, 0:1], P, RMAX).then_inc(largest_reduced, 1)

            def inverse_root(i, ready, v, out, done):
                pool.wait_ge(ready, i + 1)
                nc.gpsimd.tensor_tensor(out, v, neg_half[:, :], ALU.pow).then_inc(done, 1)

            inverse_root(0, var_ready, var[:, :], rstd[:, :], rstd_ready)

            inverse_root(1, var_ready, var[:, :], rstd[:, :], rstd_ready)
            with pool.Fori(1, NB - 1) as i:
                inverse_root(i - 1, var1_ready, var1[:, :], rstd1[:, :], rstd1_ready)
                inverse_root(i + 1, var_ready, var[:, :], rstd[:, :], rstd_ready)
            for i in (NB - 2, NB - 1):
                inverse_root(i, var1_ready, var1[:, :], rstd1[:, :], rstd1_ready)

        @block.scalar
        def _(act):
            def sequence(i):
                for c in range(NC):
                    act.wait_ge(xT_full, NC * i + c + 1)
                    nc.scalar.activation(xT_hi[:, c, :], gu[:, c, :], ACT.Copy).then_inc(hiT_done, 1)

                def gate(b):
                    act.wait_ge(gate_full, NI * i + b + 1)
                    wait_if_any(act, hidden_done, NI * i + b - 1)
                    nc.scalar.activation(silu[:, b % 2, :], gu[:, 2 * (b % 2), :], ACT.Silu,
                                         scale=gate_scale[:, b:b + 1]).then_inc(silu_done, 1)

                gate(0)
                for b in range(NI):
                    if b + 1 < NI:
                        gate(b + 1)
                    wait_if_any(act, down_step, NI * i + b - 2)
                    act.wait_ge(hidden_done, NI * i + b + 1)
                    nc.scalar.activation(hid_hi[:, b % 3, :], hidden[:, b % 2, :], ACT.Copy).then_inc(hid_hi_done, 1)

            act.wait_ge(setup_done, 1)
            sequence(0)
            with act.Fori(1, NB) as i:
                sequence(i)

        @block.vector
        def _(dve):
            steps = [0]

            def setup(ins):
                steps[0] += 1
                ins.then_inc(setup_step, 1)
                dve.wait_ge(setup_step, steps[0])

            dve.wait_ge(weights_in, 48)
            dve.wait_ge(tables_in, 48)
            for n in range(3):
                nc.vector.tensor_reduce(largest[:, n:n + 1], raw[n][:, :, :], AX.XY, ALU.max, apply_absolute_value=True)
            nc.vector.tensor_reduce(largest[:, 3:4], scales[:, 0, :], AX.X, ALU.max, apply_absolute_value=True)
            nc.vector.tensor_reduce(largest[:, 4:5], scales[:, 1, :], AX.X, ALU.max,
                                    apply_absolute_value=True).then_inc(largest_ready, 1)
            power_of_two_scales(dve, None, nc, setup, largest, largest_all[:, 0:3], power[:, 0:3], scale[:, 0:3],
                                unscale[:, 0:3], largest_ready, largest_reduced, 1)
            bound = power[:, 3:4]
            setup(nc.vector.tensor_scalar(bound, largest_all[:, 0:1], largest_all[:, 3:4], float(C), ALU.mult, ALU.mult))
            setup(nc.vector.tensor_scalar(bound, bound, largest_all[:, 1:2], largest_all[:, 4:5], ALU.mult, ALU.mult))
            setup(nc.vector.tensor_scalar(bound, bound, float(C), 2.0 ** -60, ALU.mult, ALU.max))
            setup(nc.vector.tensor_scalar(bound, bound, 2.0 ** 60, None, ALU.min))
            setup(nc.vector.tensor_scalar(bound.bitcast(I32), bound.bitcast(I32), EXPONENT_BITS, None, ALU.bitwise_and))
            setup(nc.vector.reciprocal(scale[:, 3:4], bound))
            setup(nc.vector.tensor_scalar(scale[:, 3:4], scale[:, 3:4], 2.0 ** 14, None, ALU.mult))
            setup(nc.vector.tensor_scalar(unscale[:, 3:4], bound, 2.0 ** -14, None, ALU.mult))
            nc.vector.tensor_scalar(gate_scale[:, :], scales[:, 0, :], unscale[:, 0:1], None, ALU.mult)
            nc.vector.tensor_scalar(up_scale[:, :], scales[:, 1, :], unscale[:, 1:2], scale[:, 3:4], ALU.mult, ALU.mult)
            nc.vector.tensor_scalar(down_row[:, :], down_row[:, :], unscale[:, 2:3], unscale[:, 3:4], ALU.mult, ALU.mult)
            pairs = ((gate_hi, gate_lo), (up_hi, up_lo), (down_hi, down_lo))
            for n, (hi, lo) in enumerate(pairs):
                last = nc.vector.tensor_scalar(hi[:, :, :], raw[n][:, :, :], scale[:, n:n + 1], None, ALU.mult)
            setup(last)
            for n, (hi, lo) in enumerate(pairs):
                last = nc.vector.scalar_tensor_tensor(lo[:, :, :], raw[n][:, :, :], scale[:, n:n + 1], hi[:, :, :],
                                                      ALU.mult, ALU.subtract)
            setup(last)
            for n, (hi, lo) in enumerate(pairs):
                last = nc.vector.tensor_reduce(rest[:, 1 + n:2 + n], lo[:, :, :], AX.XY, ALU.max,
                                               apply_absolute_value=True)
            setup(last)
            nc.vector.tensor_reduce(rest[:, 0:1], rest[:, 1:4], AX.X, ALU.max).then_inc(largest_ready, 1)
            dve.wait_ge(largest_reduced, 2)
            nc.vector.tensor_copy(has_rest[:, :], rest_all[:, :]).then_inc(setup_done, 1)
            dve.wait_ge(setup_done, 1)
            dve.wait_ge(consts, 3)

            def ln2(k):
                def step(ins, stats_next=False):
                    step.n += 1
                    ins.then_inc(ln_step, 1)
                    done = held(dve, 2 * k + step.n)
                    if stats_next:
                        dve.wait_ge(setup_done, 1)
                    dve.wait_ge(ln_step, done)
                step.n = 0
                dve.wait_ge(x_in, 16 * k + 16)
                for t in range(NT):
                    last = nc.vector.bn_stats(stats[:, t, :], xn[:, t, :])
                step(last, True)
                for t in range(NT):
                    last = nc.vector.bn_aggr(mv[:, t, :], stats[:, t, :])
                step(last)
                nc.vector.tensor_scalar(var[:, :], mv[:, :, 1], EPS, None, ALU.add).then_inc(var_ready, 1)
                dve.wait_ge(rstd_ready, k + 1)
                for t in range(NT):
                    last = nc.vector.tensor_scalar(xn[:, t, :], xn[:, t, :], mv[:, t, 0:1], rstd[:, t:t + 1],
                                                   ALU.subtract, ALU.mult)
                last.then_inc(xn_ready, 1)

            def finish(i):
                def step(ins, stats_next=False):
                    step.n += 1
                    ins.then_inc(end_step, 1)
                    done = held(dve, 3 * i + step.n)
                    if stats_next:
                        dve.wait_ge(setup_done, 1)
                    dve.wait_ge(end_step, done)
                step.n = 0
                dve.wait_ge(down_step, NI * (i + 1))
                for t in range(NT):
                    nc.vector.tensor_tensor(y[:, t, :], down[:, t, :], down_row[:, :], ALU.mult).then_inc(down_read, 1)
                for t in range(NT):
                    dve.wait_ge(down_read, NT * i + t + 1)
                    last = nc.vector.bn_stats(stats1[:, t, :], y[:, t, :])
                step(last, True)
                for t in range(NT):
                    last = nc.vector.bn_aggr(mv1[:, t, :], stats1[:, t, :])
                step(last)
                nc.vector.tensor_scalar(var1[:, :], mv1[:, :, 1], EPS, None, ALU.add).then_inc(var1_ready, 1)
                dve.wait_ge(rstd1_ready, i + 1)
                for t in range(NT):
                    last = nc.vector.tensor_scalar(y[:, t, :], y[:, t, :], mv1[:, t, 0:1], rstd1[:, t:t + 1],
                                                   ALU.subtract, ALU.mult)
                step(last)
                dve.wait_ge(xr_in, 16 * i + 16)
                nc.vector.tensor_tensor(xr[:, :, :], xr[:, :, :], y[:, :, :], ALU.add).then_inc(out_ready, 1)

            def sequence(i, last_sequence):
                for c in range(NC):
                    dve.wait_ge(hiT_done, NC * i + c + 1)
                    nc.vector.tensor_tensor(xT_lo[:, c, :], gu[:, c, :], xT_hi[:, c, :], ALU.subtract).then_inc(loT_done, 1)

                def product(b):
                    wait_if_any(dve, hid_hi_done, NI * i + b - 1)
                    wait_if_any(dve, hid_lo_done, NI * i + b - 1)
                    dve.wait_ge(up_full, NI * i + b + 1)
                    dve.wait_ge(silu_done, NI * i + b + 1)
                    nc.vector.scalar_tensor_tensor(hidden[:, b % 2, :], gu[:, 2 * (b % 2) + 1, :], up_scale[:, b:b + 1],
                                                   silu[:, b % 2, :], ALU.mult, ALU.mult).then_inc(hidden_done, 1)

                if not isinstance(i, int) or i > 0:
                    finish(i - 1)
                product(0)
                for b in range(NI):
                    if b + 1 < NI:
                        product(b + 1)
                    wait_if_any(dve, down_step, NI * i + b - 2)
                    dve.wait_ge(hid_hi_done, NI * i + b + 1)
                    nc.vector.tensor_tensor(hid_lo[:, b % 3, :], hidden[:, b % 2, :], hid_hi[:, b % 3, :],
                                            ALU.subtract).then_inc(hid_lo_done, 1)
                    if b == 4 and not last_sequence:
                        ln2(i + 1)

            ln2(0)
            sequence(0, False)
            with dve.Fori(1, NB - 1) as i:
                sequence(i, False)
            sequence(NB - 1, True)
            finish(NB - 1)

        @block.tensor
        def _(pe):
            def sequence(i, with_rest):
                pe.wait_ge(xn_ready, i + 1)
                wait_if_any(pe, hidden_done, NI * i)
                for c in range(NC):
                    for t in range(NT):
                        last = nc.tensor.transpose(gu[:, c, P * t:P * (t + 1)], xn[:, t, P * c:P * (c + 1)], ident[:, :])
                    last.then_inc(xT_full, 1)

                def inner(hi, lo, b, bank):
                    cols = slice(P * b, P * (b + 1))
                    for c in range(NC):
                        nc.tensor.matmul(gu[:, bank, :], hi[:, c, cols], xT_hi[:, c, :], start=c == 0, stop=False)
                        end = c == NC - 1
                        last = nc.tensor.matmul(gu[:, bank, :], hi[:, c, cols], xT_lo[:, c, :], start=False,
                                                stop=end and not with_rest)
                        if with_rest:
                            last = nc.tensor.matmul(gu[:, bank, :], lo[:, c, cols], xT_hi[:, c, :], start=False, stop=end)
                    return last

                def project_down(b):
                    pe.wait_ge(hid_lo_done, NI * i + b + 1)
                    if b == 0:
                        wait_if_any(pe, down_read, NT * i)
                    for t in range(NT):
                        rows = slice(P * t, P * (t + 1))
                        nc.tensor.matmul(down[:, t, :], hid_hi[:, b % 3, rows], down_hi[:, b, :], start=b == 0, stop=False)
                        if with_rest:
                            nc.tensor.matmul(down[:, t, :], hid_hi[:, b % 3, rows], down_lo[:, b, :], start=False,
                                             stop=False)
                        last = nc.tensor.matmul(down[:, t, :], hid_lo[:, b % 3, rows], down_hi[:, b, :], start=False,
                                                stop=b == NI - 1)
                    last.then_inc(down_step, 1)

                pe.wait_ge(loT_done, NC * (i + 1))
                for b in range(NI):
                    wait_if_any(pe, hidden_done, NI * i + b - 1)
                    inner(gate_hi, gate_lo, b, 2 * (b % 2)).then_inc(gate_full, 1)
                    inner(up_hi, up_lo, b, 2 * (b % 2) + 1).then_inc(up_full, 1)
                    if b >= 2:
                        project_down(b - 2)
                project_down(NI - 2)
                project_down(NI - 1)

            pe.wait_ge(setup_done, 1)
            pe.wait_ge(consts, 3)
            any_rest = pe.alloc_register("any_rest")
            pe.reg_load(any_rest, has_rest[0:1, 0:1].bitcast(I32))
            with pe.If_ne(any_rest, 0):
                sequence(0, True)
                with pe.Fori(1, NB) as i:
                    sequence(i, True)
            with pe.Else():
                sequence(0, False)
                with pe.Fori(1, NB) as i:
                    sequence(i, False)


def rope_tables():
    frame, gamma = 144, 0.5
    theta = (np.float32(10000.0) ** (-np.arange(0, DH, 2, dtype=np.float32) / np.float32(DH))).astype(np.float32)
    tok = np.arange(T)
    temporal = np.floor((tok // frame).astype(np.float32) * gamma).astype(np.int32)
    angle = (tok.astype(np.float32)[:, None] * theta).astype(np.float64)
    angle += (temporal.astype(np.float32)[:, None] * theta).astype(np.float64)
    cos = np.concatenate([np.cos(angle), np.cos(angle)], 1).astype(np.float32)
    sin = np.concatenate([-np.sin(angle), np.sin(angle)], 1).astype(np.float32)
    return [np.ascontiguousarray(a.reshape(NT, P, DH).transpose(1, 0, 2)) for a in (cos, sin)]


def by_partition(a, tiles):
    return np.ascontiguousarray(a.reshape(tiles, P, -1).transpose(1, 0, 2))


def kernel(**inputs):
    import concourse.bacc as bacc
    from concourse.bass_utils import run_bass_kernel_spmd

    get = {n.removeprefix("L0_"): np.asarray(a) for n, a in inputs.items()}
    arrays = {"x": np.ascontiguousarray(get["attn_hidden_states"].reshape(NB, NT, P, C).transpose(0, 2, 1, 3))}
    for n in "qkvo":
        arrays[f"w{n}T"] = by_partition(get[f"attn_W{n}"].T, NC)
        arrays[f"b{n}"] = np.ascontiguousarray(np.broadcast_to(get[f"attn_b{n}"], (P, C)))
    arrays["rope_cos"], arrays["rope_sin"] = rope_tables()
    arrays["gateT"] = by_partition(get["ffn_gate_w"].T, NC)
    arrays["upT"] = by_partition(get["ffn_up_w"].T, NC)
    arrays["downT"] = by_partition(get["ffn_down_w"].T, NI)
    arrays["gate_s"] = np.ascontiguousarray(get["ffn_gate_s"].reshape(NI, P).T)
    arrays["up_s"] = np.ascontiguousarray(get["ffn_up_s"].reshape(NI, P).T)
    arrays["down_s"] = np.ascontiguousarray(np.broadcast_to(get["ffn_down_s"], (P, C)))

    nc = bacc.Bacc("TRN2", target_bir_lowering=False, num_devices=1)
    ap = {n: nc.dram_tensor(n, a.shape, mybir.dt.from_np(a.dtype), kind="ExternalInput").ap() for n, a in arrays.items()}
    x1 = nc.dram_tensor("x1", (NB, P, NT, C), F32, kind="Internal").ap()
    out = nc.dram_tensor("out", (NB, P, NT, C), F32, kind="ExternalOutput").ap()
    attention_phase(nc, ap["x"], [ap[f"w{n}T"] for n in "qkvo"], [ap[f"b{n}"] for n in "qkvo"],
                    ap["rope_cos"], ap["rope_sin"], x1)
    ffn_phase(nc, x1, ap["gateT"], ap["upT"], ap["downT"], ap["gate_s"], ap["up_s"], ap["down_s"], out)
    r = run_bass_kernel_spmd(nc, [arrays], core_ids=[0])
    return r.results[0]["out"].transpose(0, 2, 1, 3).reshape(NB, T, C)
```

```python
from contextlib import ExitStack

import numpy as np

import concourse.bass as bass
from concourse import mybir

F32 = mybir.dt.float32
F16 = mybir.dt.float16
I32 = mybir.dt.int32
ALU = mybir.AluOpType
ACT = mybir.ActivationFunctionType
AX = mybir.AxisListType
RMAX = bass.bass_isa.ReduceOp.max

P = 128
NB, T, C = 16, 512, 512
H, DH = 32, 16
NT = T // P
NC = C // P
INTER = 1408
NI = INTER // P
EPS = 1e-5
EXPONENT_BITS = 0x7F800000

HG = 4
NG = H // HG
SLOT = 64
SHIFT_UNIT = 32768.0
NU = 2 * NT


def held(engine, value):
    return value if isinstance(value, int) else engine.to_reg(value)


def wait_if_any(engine, semaphore, value):
    if not isinstance(value, int) or value > 0:
        engine.wait_ge(semaphore, value)


def power_of_two_scales(dve, nc, link, largest_all, power, scale, unscale, reduced):
    dve.wait_ge(reduced, 1)
    link(nc.vector.tensor_scalar(power, largest_all, 2.0 ** -60, 2.0 ** 60, ALU.max, ALU.min))
    link(nc.vector.tensor_scalar(power.bitcast(I32), power.bitcast(I32), EXPONENT_BITS, None, ALU.bitwise_and))
    link(nc.vector.reciprocal(scale, power))
    link(nc.vector.tensor_scalar(scale, scale, 4.0, None, ALU.mult))
    link(nc.vector.tensor_scalar(unscale, power, 0.25, None, ALU.mult))


def attention_phase(nc, x, wT, bias, rope_cos, rope_sin, x1):
    ctx = ExitStack()
    with ctx:
        def sb(name, shape, dt=F32):
            return ctx.enter_context(nc.sbuf_tensor(name, shape, dt))

        def pb(name, shape, dt=F32):
            return ctx.enter_context(nc.psum_tensor(name, shape, dt))

        def sem(name):
            return ctx.enter_context(nc.semaphore(name))

        w_hi = sb("w_hi", [P, 4, NC, C], F16)
        w_lo = sb("w_lo", [P, 4, NC, C], F16)
        bias_sb = sb("bias_sb", [P, 4, C])
        cos_sb = sb("cos_sb", [P, NT, DH])
        sin_sb = sb("sin_sb", [P, NT, DH])
        ident = sb("ident", [P, P])
        ident16 = sb("ident16", [P, P], F16)
        causal = sb("causal", [P, T])
        neg_half = sb("neg_half", [P, NT])
        largest = sb("largest", [P, 8])
        largest_all = sb("largest_all", [P, 4])
        power = sb("power", [P, 4])
        scale = sb("scale", [P, 4])
        unscale = sb("unscale", [P, 4])
        exp_scale = sb("exp_scale", [P, 1])
        out_unscale = sb("out_unscale", [P, 1])

        xn = sb("xn", [P, NT, C])
        xr = sb("xr", [P, NT, C])
        xT_hi = sb("xT_hi", [P, NC, T], F16)
        xT_lo = sb("xT_lo", [P, NC, T], F16)
        aT_hi = sb("aT_hi", [P, NC, T], F16)
        aT_lo = sb("aT_lo", [P, NC, T], F16)
        qs = sb("qs", [P, NT, H, SLOT], F16)
        ks = sb("ks", [P, NT, H, SLOT], F16)
        vs = sb("vs", [P, NT, H, 32])
        biased = sb("biased", [P, 2, C])
        turned = sb("turned", [P, 2, C])
        roped = sb("roped", [P, 2, C])
        qT = sb("qT", [P, 2, 2, T], F16)
        qmT = sb("qmT", [P, 2, 2, T], F16)
        kT = sb("kT", [P, 3, 2, T], F16)
        probs = sb("probs", [P, NT, HG, T])
        row_max = sb("row_max", [P, 2, NT, HG])
        shift = sb("shift", [P, NT, HG])
        oT = sb("oT", [P, T])
        recip = sb("recip", [P, NT, HG])
        attn = sb("attn", [P, NT, C])
        stats = sb("stats", [P, NT, 6])
        mv = sb("mv", [P, NT, 2])
        var = sb("var", [P, NT])
        rstd = sb("rstd", [P, NT])
        stats1 = sb("stats1", [P, NT, 6])
        mv1 = sb("mv1", [P, NT, 2])
        var1 = sb("var1", [P, NT])
        rstd1 = sb("rstd1", [P, NT])

        ring = pb("ring", [P, 4, 512])
        narrow = pb("narrow", [P, 2, 512])
        av = pb("av", [P, T])
        turn = pb("turn", [P, T])
        turn16 = turn[:, :].bitcast(F16).rearrange("p (a t) -> p a t", a=2)

        weights_in = sem("weights_in")
        tables_in = sem("tables_in")
        consts = sem("consts")
        largest_ready = sem("largest_ready")
        largest_reduced = sem("largest_reduced")
        setup_step = sem("setup_step")
        setup_done = sem("setup_done")
        x_in = sem("x_in")
        xr_in = sem("xr_in")
        x1_out = sem("x1_out")
        var_ready = sem("var_ready")
        rstd_ready = sem("rstd_ready")
        ln1_step = sem("ln1_step")
        xn_ready = sem("xn_ready")
        narrow_full = sem("narrow_full")
        narrow_free = sem("narrow_free")
        xT_hi_done = sem("xT_hi_done")
        aT_hi_done = sem("aT_hi_done")
        k_and_q_biased = sem("k_and_q_biased")
        turned_done = sem("turned_done")
        roped_done = sem("roped_done")
        qk_hi = sem("qk_hi")
        qk_lo = sem("qk_lo")
        turn_full = sem("turn_full")
        turn_read_act = sem("turn_read_act")
        turn_read_dve = sem("turn_read_dve")
        shift_step = sem("shift_step")
        shift_ready = sem("shift_ready")
        v_full = sem("v_full")
        v_read = sem("v_read")
        st_full = sem("st_full")
        st_read = sem("st_read")
        masked = sem("masked")
        av_done = sem("av_done")
        oT_ready = sem("oT_ready")
        recip_done = sem("recip_done")
        out_full = sem("out_full")
        out_read = sem("out_read")
        out_step = sem("out_step")
        var1_ready = sem("var1_ready")
        rstd1_ready = sem("rstd1_ready")
        x1_ready = sem("x1_ready")

        NS = NG * NU
        AHEAD = NU + 5
        START = -2 * NU
        FRONT = NC + 2 * NT
        FRONT_AT = NS - AHEAD
        FRONT_SLOTS = NS - FRONT_AT - 3
        N_NARROW = FRONT + 2 * NS
        V_AT = (-14, -12, -9, -6)
        A_AT = {3 * NU + 3: 0, 5 * NU + 3: 1, 7 * NU + 3: 2}

        def transposes_at(w):
            g, u = divmod(w, NU)
            out = []
            if u == 0 and g + 2 < NG:
                out.append(("q", g + 2))
            if u == 1 and g + 2 < NG:
                out.append(("k", g + 2))
            if w in A_AT:
                out.append(("a", A_AT[w]))
            if u == 5 and g + 1 < NG and g + 1 >= 0:
                out.append(("m", g + 1))
            if u == 6 and g >= 1:
                out.append(("o", g - 1))
            return out

        turn_uses = [use for w in range(START, NS) for use in transposes_at(w)] + [("o", NG - 1), ("a", NC - 1)]
        N_TURN = len(turn_uses)
        BY_ACT = sum(kind in "qkm" for kind, _ in turn_uses)
        BY_DVE = N_TURN - BY_ACT

        def weighed_at(w):
            n = (w - 5) // 2
            return n if w >= 5 and w % 2 == 1 and n < NG * NT else None

        block = ctx.enter_context(nc.Block())

        @block.sync
        def _(sp):
            for n in range(4):
                sp.dma_start(probs[:, n, :, :], wT[n]).then_inc(weights_in, 16)
            for n in range(4):
                sp.dma_start(bias_sb[:, n, :], bias[n]).then_inc(tables_in, 16)
            sp.dma_start(cos_sb[:, :, :], rope_cos).then_inc(tables_in, 16)
            sp.dma_start(sin_sb[:, :, :], rope_sin).then_inc(tables_in, 16)
            sp.dma_start(xn[:, :, :], x[0, :, :, :]).then_inc(x_in, 16)
            sp.dma_start(xr[:, :, :], x[0, :, :, :]).then_inc(xr_in, 16)

            def sequence(i, last):
                if not last:
                    sp.wait_ge(narrow_full, N_NARROW * i + NC)
                    sp.dma_start(xn[:, :, :], x[i + 1, :, :, :]).then_inc(x_in, 16)
                if not isinstance(i, int) or i > 0:
                    sp.wait_ge(x1_ready, i)
                    sp.dma_start(x1[i - 1, :, :, :], xr[:, :, :]).then_inc(x1_out, 16)
                    sp.wait_ge(x1_out, 16 * i)
                    sp.dma_start(xr[:, :, :], x[i, :, :, :]).then_inc(xr_in, 16)

            sequence(0, False)
            with sp.Fori(1, NB - 1) as i:
                sequence(i, False)
            sequence(NB - 1, True)
            sp.wait_ge(x1_ready, NB)
            sp.dma_start(x1[NB - 1, :, :, :], xr[:, :, :]).then_inc(x1_out, 16)
            sp.wait_ge(x1_out, 16 * NB)

        @block.gpsimd
        def _(pool):
            nc.gpsimd.memset(ident[:, :], 0.0).then_inc(consts, 1)
            nc.gpsimd.memset(ident16[:, :], 0.0).then_inc(consts, 1)
            nc.gpsimd.memset(causal[:, :], 0.0).then_inc(consts, 1)
            nc.gpsimd.memset(neg_half[:, :], -0.5).then_inc(consts, 1)
            pool.wait_ge(consts, 4)
            for m in (ident, ident16):
                nc.gpsimd.affine_select(out=m[:, :], in_=m[:, :], compare_op=ALU.not_equal, fill=1.0, base=0,
                                        pattern=[[-1, P]], channel_multiplier=1).then_inc(consts, 1)
            tri = causal[:, T - P:T]
            nc.gpsimd.affine_select(out=tri, in_=tri, compare_op=ALU.is_ge, fill=-1e38, base=0,
                                    pattern=[[-1, P]], channel_multiplier=1).then_inc(consts, 1)
            pool.wait_ge(largest_ready, 1)
            nc.gpsimd.partition_all_reduce(largest_all[:, :], largest[:, 0:4], P, RMAX).then_inc(largest_reduced, 1)

            def inverse_root(i, ready, v, out, done):
                pool.wait_ge(ready, i + 1)
                nc.gpsimd.tensor_tensor(out, v, neg_half[:, :], ALU.pow).then_inc(done, 1)

            def turn_pairs(i, n):
                t = n % NT
                pool.wait_ge(k_and_q_biased, 2 * NT * i + n + 1)
                a = biased[:, n % 2, :].rearrange("p (h d) -> p h d", h=H)
                o = turned[:, n % 2, :].rearrange("p (h d) -> p h d", h=H)
                s = sin_sb[:, t:t + 1, :]
                half = DH // 2
                nc.gpsimd.tensor_tensor(o[:, :, 0:half], a[:, :, half:DH],
                                        s[:, :, 0:half].broadcast_to([P, H, half]), ALU.mult)
                nc.gpsimd.tensor_tensor(o[:, :, half:DH], a[:, :, 0:half],
                                        s[:, :, half:DH].broadcast_to([P, H, half]), ALU.mult).then_inc(turned_done, 1)

            def mask(i, n):
                kt = n % NT
                exps_done = held(pool, NS * i + 2 * n + 2)
                pool.wait_ge(consts, 7)
                pool.wait_ge(st_read, exps_done)
                d = probs[:, kt, :, P * kt:P * kt + P]
                nc.gpsimd.affine_select(out=d, in_=d, compare_op=ALU.is_ge, fill=0.0, base=0,
                                        pattern=[[0, HG], [1, P]], channel_multiplier=-1).then_inc(masked, 1)

            def sequence(i, last):
                for w in range(2, NS + 1):
                    if w % 2 == 0:
                        mask(i, w // 2 - 1)
                    if not last and w == FRONT_AT - 2:
                        inverse_root(i + 1, var_ready, var[:, :], rstd[:, :], rstd_ready)
                    n = w - FRONT_AT - NC - 1
                    if not last and 0 <= n < FRONT_SLOTS - NC:
                        turn_pairs(i + 1, n)
                if not last:
                    for n in range(FRONT_SLOTS - NC, 2 * NT):
                        turn_pairs(i + 1, n)
                inverse_root(i, var1_ready, var1[:, :], rstd1[:, :], rstd1_ready)

            inverse_root(0, var_ready, var[:, :], rstd[:, :], rstd_ready)
            for n in range(2 * NT):
                turn_pairs(0, n)
            with pool.Fori(0, NB - 1) as i:
                sequence(i, False)
            sequence(NB - 1, True)

        @block.scalar
        def _(act):
            def high_of_x(i, c):
                act.wait_ge(narrow_full, N_NARROW * i + c + 1)
                nc.scalar.activation(xT_hi[:, c, :], narrow[:, c % 2, :], ACT.Copy).then_inc(xT_hi_done, 1)

            def high_of_k_or_q(i, n):
                t = n % NT
                act.wait_ge(roped_done, 2 * NT * i + n + 1)
                src = roped[:, n % 2, :].rearrange("p (h o d) -> p h o d", h=H, o=1).broadcast_to([P, H, 2, DH])
                dst = (ks if n < NT else qs)[:, t, :, :].rearrange("p h (s d) -> p h s d", d=DH)
                dst = dst[:, :, 0:2, :] if n < NT else dst[:, :, 0:3:2, :]
                nc.scalar.activation(dst, src, ACT.Copy).then_inc(qk_hi, 1)

            def front(i, f):
                if f < NC:
                    high_of_x(i, f)
                elif f > NC:
                    high_of_k_or_q(i, f - NC - 1)

            def high_of_attention(i, c):
                act.wait_ge(turn_full, N_TURN * i + turn_uses.index(("a", c)) + 1)
                nc.scalar.activation(aT_hi[:, c, :], turn[:, :], ACT.Copy).then_inc(aT_hi_done, 1)

            def read_transposed(i, kind, g):
                act.wait_ge(turn_full, N_TURN * i + turn_uses.index((kind, g)) + 1)
                dst = {"q": qT[:, g % 2, :, :], "m": qmT[:, g % 2, :, :], "k": kT[:, g % 3, :, :]}[kind]
                nc.scalar.activation(dst, turn16, ACT.Copy).then_inc(turn_read_act, 1)

            def exponentials(i, w):
                g, u = divmod(w, NU)
                kt, pair = divmod(u, 2)
                if g > 0:
                    act.wait_ge(av_done, NG * NT * i + NT * (g - 1) + kt + 1)
                act.wait_ge(st_full, NS * i + w + 1)
                bank = 2 * (w % 2)
                nc.scalar.activation(probs[:, kt, 2 * pair:2 * pair + 2, P * kt:T], ring[:, bank:bank + 2, 0:T - P * kt],
                                     ACT.Exp, scale=exp_scale[:, 0:1]).then_inc(st_read, 1)

            def read_weighed(i, g):
                act.wait_ge(av_done, NG * NT * i + NT * (g + 1))
                nc.scalar.activation(oT[:, :], av[:, :], ACT.Copy).then_inc(oT_ready, 1)

            def sequence(i, last):
                for w in range(START, NS):
                    g, u = divmod(w, NU)
                    if u == 4 and g >= 1:
                        read_weighed(i, g - 1)
                    if w >= 0:
                        exponentials(i, w)
                    for kind, n in transposes_at(w):
                        if kind in "qkm":
                            read_transposed(i, kind, n)
                        elif kind == "a":
                            high_of_attention(i, n)
                    if not last and 0 <= w - FRONT_AT < FRONT_SLOTS:
                        front(i + 1, w - FRONT_AT)
                read_weighed(i, NG - 1)
                if not last:
                    for f in range(FRONT_SLOTS, FRONT):
                        front(i + 1, f)
                high_of_attention(i, NC - 1)
                if not last:
                    high_of_k_or_q(i + 1, 2 * NT - 1)

            act.wait_ge(setup_done, 1)
            for f in range(FRONT):
                front(0, f)
            high_of_k_or_q(0, 2 * NT - 1)
            with act.Fori(0, NB - 1) as i:
                sequence(i, False)
            sequence(NB - 1, True)

        @block.vector
        def _(dve):
            steps = [0]

            def setup(ins):
                steps[0] += 1
                ins.then_inc(setup_step, 1)
                dve.wait_ge(setup_step, steps[0])

            nc.vector.memset(qs[:, :, :, :], 0.0)
            nc.vector.memset(ks[:, :, :, :], 0.0)
            setup(nc.vector.memset(vs[:, :, :, :], 0.0))
            nc.vector.memset(ks[:, :, :, 3 * DH:3 * DH + 2], SHIFT_UNIT)
            setup(nc.vector.memset(vs[:, :, :, DH:DH + 1], 1.0))
            dve.wait_ge(weights_in, 64)
            dve.wait_ge(tables_in, 96)
            for n in range(4):
                nc.vector.tensor_reduce(largest[:, n:n + 1], probs[:, n, :, :], AX.XY, ALU.max,
                                        apply_absolute_value=True)
                last = nc.vector.tensor_reduce(largest[:, 4 + n:5 + n], bias_sb[:, n, :], AX.X, ALU.max,
                                               apply_absolute_value=True)
            setup(last)
            setup(nc.vector.tensor_scalar(largest[:, 4:8], largest[:, 4:8], 1.0 / C, None, ALU.mult))
            nc.vector.tensor_tensor(largest[:, 0:4], largest[:, 0:4], largest[:, 4:8], ALU.max).then_inc(largest_ready, 1)
            power_of_two_scales(dve, nc, setup, largest_all[:, :], power[:, :], scale[:, :],
                                unscale[:, :], largest_reduced)
            for n in range(3):
                nc.vector.tensor_scalar(bias_sb[:, n, :], bias_sb[:, n, :], scale[:, n:n + 1], None, ALU.mult)
            nc.vector.tensor_scalar(exp_scale[:, :], unscale[:, 0:1], unscale[:, 1:2], DH ** -0.5, ALU.mult, ALU.mult)
            nc.vector.tensor_scalar(out_unscale[:, :], unscale[:, 2:3], unscale[:, 3:4], None, ALU.mult)
            for n in range(4):
                last = nc.vector.tensor_scalar(w_hi[:, n, :, :], probs[:, n, :, :], scale[:, n:n + 1], None, ALU.mult)
            setup(last)
            for n in range(4):
                last = nc.vector.scalar_tensor_tensor(w_lo[:, n, :, :], probs[:, n, :, :], scale[:, n:n + 1],
                                                      w_hi[:, n, :, :], ALU.mult, ALU.subtract)
            last.then_inc(setup_done, 1)
            dve.wait_ge(setup_done, 1)
            dve.wait_ge(consts, 7)

            def await_step(step_semaphore, value, stats_next=False):
                done = held(dve, value)
                if stats_next:
                    dve.wait_ge(setup_done, 1)
                dve.wait_ge(step_semaphore, done)

            def statistics_of_x(i, t):
                arrived = held(dve, 16 * (i + 1))
                dve.wait_ge(setup_done, 1)
                dve.wait_ge(x_in, arrived)
                nc.vector.bn_stats(stats[:, t, :], xn[:, t, :]).then_inc(ln1_step, 1)

            def variance_of_x(i):
                await_step(ln1_step, (NT + 1) * i + NT, True)
                for t in range(NT):
                    last = nc.vector.bn_aggr(mv[:, t, :], stats[:, t, :])
                last.then_inc(ln1_step, 1)

            def shifted_variance_of_x(i):
                await_step(ln1_step, (NT + 1) * (i + 1))
                nc.vector.tensor_scalar(var[:, :], mv[:, :, 1], EPS, None, ALU.add).then_inc(var_ready, 1)

            def normalise_x(i):
                dve.wait_ge(rstd_ready, i + 1)
                for t in range(NT):
                    last = nc.vector.tensor_scalar(xn[:, t, :], xn[:, t, :], mv[:, t, 0:1], rstd[:, t:t + 1],
                                                   ALU.subtract, ALU.mult)
                last.then_inc(xn_ready, 1)

            def low_of_x(i, c):
                dve.wait_ge(xT_hi_done, NC * i + c + 1)
                nc.vector.tensor_tensor(xT_lo[:, c, :], narrow[:, c % 2, :], xT_hi[:, c, :],
                                        ALU.subtract).then_inc(narrow_free, 1)

            def low_of_attention(i, c):
                dve.wait_ge(aT_hi_done, NC * i + c + 1)
                nc.vector.tensor_tensor(aT_lo[:, c, :], turn[:, :], aT_hi[:, c, :],
                                        ALU.subtract).then_inc(turn_read_dve, 1)

            def bias_and_cosine(i, n):
                t, which = n % NT, 1 - n // NT
                wait_if_any(dve, turned_done, 2 * NT * i + n - 1)
                dve.wait_ge(narrow_full, N_NARROW * i + NC + n + 1)
                nc.vector.tensor_tensor(biased[:, n % 2, :], narrow[:, (NC + n) % 2, :], bias_sb[:, which, :],
                                        ALU.add).then_inc(narrow_free, 1)
                wait_if_any(dve, qk_hi, 2 * NT * i + n - 1)
                await_step(narrow_free, N_NARROW * i + NC + n + 1)
                r = roped[:, n % 2, :].rearrange("p (h d) -> p h d", h=H)
                nc.vector.tensor_tensor(r, biased[:, n % 2, :].rearrange("p (h d) -> p h d", h=H),
                                        cos_sb[:, t:t + 1, :].broadcast_to([P, H, DH]),
                                        ALU.mult).then_inc(k_and_q_biased, 1)

            def add_sine(i, n):
                dve.wait_ge(turned_done, 2 * NT * i + n + 1)
                nc.vector.tensor_tensor(roped[:, n % 2, :], roped[:, n % 2, :], turned[:, n % 2, :],
                                        ALU.add).then_inc(roped_done, 1)

            def low_of_k_or_q(i, n):
                t = n % NT
                dst, at = (ks, 2 * DH) if n < NT else (qs, DH)
                dve.wait_ge(qk_hi, 2 * NT * i + n + 1)
                nc.vector.tensor_tensor(dst[:, t, :, at:at + DH],
                                        roped[:, n % 2, :].rearrange("p (h d) -> p h d", h=H),
                                        dst[:, t, :, 0:DH], ALU.subtract).then_inc(qk_lo, 1)

            def front(i, f):
                n = f - NC
                if n < 0:
                    low_of_x(i, f)
                    return
                if n >= 2:
                    low_of_k_or_q(i, n - 2)
                if n < 2 * NT:
                    bias_and_cosine(i, n)
                if n == NT:
                    nc.vector.memset(qs[:, :, :, 3 * DH:3 * DH + 2], 0.0)
                if 1 <= n <= 2 * NT:
                    add_sine(i, n - 1)

            def bias_v(i, t):
                dve.wait_ge(v_full, NT * i + t + 1)
                nc.vector.tensor_tensor(vs[:, t, :, 0:DH], ring[:, t, :].rearrange("p (h d) -> p h d", h=H),
                                        bias_sb[:, 2, :].rearrange("p (h d) -> p h d", h=H),
                                        ALU.add).then_inc(v_read, 1)

            def maximum(i, s, j):
                g, u = divmod(s, NU)
                qt, pair = divmod(u, 2)
                n = P * (qt + 1)
                filled = held(dve, N_NARROW * i + FRONT + 2 * s + j + 1)
                dve.wait_ge(consts, 7)
                dve.wait_ge(narrow_full, filled)
                nc.vector.tensor_tensor_reduce(
                    out=narrow[:, j, 0:n], in0=narrow[:, j, 0:n], in1=causal[:, T - n:T], scale=1.0,
                    scalar=-3e38, op0=ALU.add, op1=ALU.max,
                    accum_out=row_max[:, g % 2, qt, 2 * pair + j:2 * pair + j + 1]).then_inc(narrow_free, 1)

            def maxima_beside_q(i, g, part):
                m = qs[:, :, HG * g:HG * (g + 1), :]
                if part == 0:
                    await_step(narrow_free, N_NARROW * i + FRONT + 2 * NU * (g + 1))
                    nc.vector.tensor_scalar(shift[:, :, :], row_max[:, g % 2, :, :], -1.0 / SHIFT_UNIT, None,
                                            ALU.mult).then_inc(shift_step, 1)
                elif part == 1:
                    await_step(shift_step, 2 * NG * i + 2 * g + 1)
                    nc.vector.tensor_copy(m[:, :, :, 3 * DH], shift[:, :, :]).then_inc(shift_step, 1)
                else:
                    await_step(shift_step, 2 * NG * i + 2 * g + 2)
                    nc.vector.tensor_tensor(m[:, :, :, 3 * DH + 1], shift[:, :, :], m[:, :, :, 3 * DH],
                                            ALU.subtract).then_inc(shift_ready, 1)

            def reciprocal_of_sums(i, g):
                dve.wait_ge(turn_full, N_TURN * i + turn_uses.index(("o", g)) + 1)
                o = turn[:, :].rearrange("p (t h c) -> p t h c", t=NT, c=32)
                nc.vector.reciprocal(recip[:, :, :], o[:, :, :, DH]).then_inc(recip_done, 1)

            def divide_by_sums(i, g):
                await_step(recip_done, NG * i + g + 1)
                o = turn[:, :].rearrange("p (t h c) -> p t h c", t=NT, c=32)
                r = recip[:, :, :].rearrange("p t (h o) -> p t h o", o=1).broadcast_to([P, NT, HG, DH])
                dst = attn[:, :, HG * DH * g:HG * DH * (g + 1)].rearrange("p t (h d) -> p t h d", h=HG)
                nc.vector.tensor_tensor(dst, o[:, :, :, 0:DH], r, ALU.mult).then_inc(turn_read_dve, 1)

            def projected(i):
                for t in range(NT):
                    dve.wait_ge(out_full, NT * i + t + 1)
                    nc.vector.scalar_tensor_tensor(attn[:, t, :], ring[:, t, :], out_unscale[:, 0:1],
                                                   bias_sb[:, 3, :], ALU.mult, ALU.add).then_inc(out_read, 1)
                for t in range(NT):
                    await_step(out_read, NT * i + t + 1, True)
                    last = nc.vector.bn_stats(stats1[:, t, :], attn[:, t, :])
                last.then_inc(out_step, 1)
                await_step(out_step, (2 + NT) * i + 1, True)
                for t in range(NT):
                    last = nc.vector.bn_aggr(mv1[:, t, :], stats1[:, t, :])
                last.then_inc(out_step, 1)
                await_step(out_step, (2 + NT) * i + 2)
                nc.vector.tensor_scalar(var1[:, :], mv1[:, :, 1], EPS, None, ALU.add).then_inc(var1_ready, 1)

            def normalise_projected(i, t):
                if t == 0:
                    dve.wait_ge(rstd1_ready, i + 1)
                nc.vector.tensor_scalar(attn[:, t, :], attn[:, t, :], mv1[:, t, 0:1], rstd1[:, t:t + 1],
                                        ALU.subtract, ALU.mult).then_inc(out_step, 1)

            def residual(i, t):
                if t == 0:
                    dve.wait_ge(xr_in, 16 * (i + 1))
                await_step(out_step, (2 + NT) * i + 3 + t)
                last = nc.vector.tensor_tensor(xr[:, t, :], xr[:, t, :], attn[:, t, :], ALU.add)
                if t == NT - 1:
                    last.then_inc(x1_ready, 1)

            def sequence(i, last):
                for w in range(START, NS):
                    g, u = divmod(w, NU)
                    s = w + AHEAD
                    if 0 <= s < NS:
                        maximum(i, s, 0)
                    if s % NU == 0 and 0 < s <= NS:
                        maxima_beside_q(i, s // NU - 1, 0)
                    if s % NU == 1 and 1 < s <= NS + 1:
                        maxima_beside_q(i, s // NU - 1, 2)
                    if ("o", g - 1) in transposes_at(w - 1):
                        reciprocal_of_sums(i, g - 1)
                    if w in V_AT:
                        bias_v(i, V_AT.index(w))
                    if 0 <= s < NS:
                        maximum(i, s, 1)
                    if s % NU == 0 and 0 < s <= NS:
                        maxima_beside_q(i, s // NU - 1, 1)
                    if ("o", g - 1) in transposes_at(w - 1):
                        divide_by_sums(i, g - 1)
                    if w in A_AT:
                        low_of_attention(i, A_AT[w])
                    if (not isinstance(i, int) or i > 0) and -AHEAD <= w < -AHEAD + 2 * NT:
                        t, part = divmod(w + AHEAD, 2)
                        (normalise_projected, residual)[part](i - 1, t)
                    if not last:
                        f = w - FRONT_AT
                        if -8 <= f < -4:
                            statistics_of_x(i + 1, f + 8)
                        if f == -4:
                            variance_of_x(i + 1)
                        if f == -3:
                            shifted_variance_of_x(i + 1)
                        if f == -1:
                            normalise_x(i + 1)
                        if 0 <= f < FRONT_SLOTS:
                            front(i + 1, f)
                if not last:
                    front(i + 1, FRONT_SLOTS)
                reciprocal_of_sums(i, NG - 1)
                divide_by_sums(i, NG - 1)
                if not last:
                    front(i + 1, FRONT_SLOTS + 1)
                low_of_attention(i, NC - 1)
                if not last:
                    front(i + 1, FRONT)
                    front(i + 1, FRONT + 1)
                projected(i)

            for t in range(NT):
                statistics_of_x(0, t)
            variance_of_x(0)
            shifted_variance_of_x(0)
            normalise_x(0)
            for f in range(FRONT + 2):
                front(0, f)
            sequence(0, False)
            with dve.Fori(1, NB - 1) as i:
                sequence(i, False)
            sequence(NB - 1, True)
            for t in range(NT):
                normalise_projected(NB - 1, t)
            for t in range(NT):
                residual(NB - 1, t)

        @block.tensor
        def _(pe):
            def three_products(out, a_hi, a_lo, b_hi, b_lo, first, last):
                nc.tensor.matmul(out, a_hi, b_hi, start=first, stop=False)
                nc.tensor.matmul(out, a_hi, b_lo, start=False, stop=False)
                return nc.tensor.matmul(out, a_lo, b_hi, start=False, stop=last)

            def project(out, hi, lo, w, t, channel_tiles):
                for c in channel_tiles:
                    last = three_products(out, hi[:, c, P * t:P * (t + 1)], lo[:, c, P * t:P * (t + 1)],
                                          w_hi[:, w, c, :], w_lo[:, w, c, :], c == 0, c == NC - 1)
                return last

            def front(i, f):
                if f == 0:
                    pe.wait_ge(xn_ready, i + 1)
                if f == NC:
                    pe.wait_ge(narrow_free, N_NARROW * i + NC)
                wait_if_any(pe, narrow_free, N_NARROW * i + f - 1)
                bank = narrow[:, f % 2, :]
                if f < NC:
                    for t in range(NT):
                        last = nc.tensor.transpose(bank[:, P * t:P * (t + 1)], xn[:, t, P * f:P * (f + 1)], ident[:, :])
                else:
                    n = f - NC
                    last = project(bank, xT_hi, xT_lo, 1 - n // NT, n % NT, range(NC))
                last.then_inc(narrow_full, 1)

            def transposed(i, kind, n):
                use = turn_uses.index((kind, n))
                if use > 0:
                    before = turn_uses[:use]
                    by_act = sum(k in "qkm" for k, _ in before)
                    if before[-1][0] in "qkm":
                        pe.wait_ge(turn_read_act, BY_ACT * i + by_act)
                    else:
                        pe.wait_ge(turn_read_dve, BY_DVE * i + use - by_act)
                else:
                    wait_if_any(pe, turn_read_dve, BY_DVE * i)
                if kind in "qkm":
                    if kind == "m":
                        pe.wait_ge(shift_ready, NG * i + n + 1)
                    elif n == 0:
                        pe.wait_ge(qk_lo, 2 * NT * (i + 1))
                    src = ks if kind == "k" else qs
                    for pair in range(2):
                        for t in range(NT):
                            h = HG * n + 2 * pair
                            last = nc.tensor.transpose(turn16[:, pair, P * t:P * (t + 1)],
                                                       src[:, t, h:h + 2, :].rearrange("p h s -> p (h s)"), ident16[:, :])
                elif kind == "o":
                    pe.wait_ge(oT_ready, NG * i + n + 1)
                    for t in range(NT):
                        last = nc.tensor.transpose(turn[:, P * t:P * (t + 1)], oT[:, P * t:P * (t + 1)], ident[:, :])
                else:
                    groups = 2 * n + 2
                    tiles = n
                    pe.wait_ge(turn_read_dve, BY_DVE * i + groups + tiles)
                    for t in range(NT):
                        last = nc.tensor.transpose(turn[:, P * t:P * (t + 1)], attn[:, t, P * n:P * (n + 1)], ident[:, :])
                last.then_inc(turn_full, 1)

            def score(i, s, j):
                g, u = divmod(s, NU)
                qt, pair = divmod(u, 2)
                if u == 0 and j == 0:
                    use = turn_uses.index(("k", g)) + 1
                    pe.wait_ge(turn_read_act, BY_ACT * i + sum(k in "qkm" for k, _ in turn_uses[:use]))
                wait_if_any(pe, narrow_free, N_NARROW * i + FRONT + 2 * s + j - 1)
                rows = slice(SLOT * j, SLOT * (j + 1))
                nc.tensor.matmul(narrow[:, j, 0:P * (qt + 1)], qT[rows, g % 2, pair, P * qt:P * (qt + 1)],
                                 kT[rows, g % 3, pair, 0:P * (qt + 1)], start=True, stop=True).then_inc(narrow_full, 1)

            def score_transposed(i, w):
                g, u = divmod(w, NU)
                kt, pair = divmod(u, 2)
                if u == 0:
                    use = turn_uses.index(("m", g)) + 1
                    pe.wait_ge(turn_read_act, BY_ACT * i + sum(k in "qkm" for k, _ in turn_uses[:use]))
                if w < 2:
                    pe.wait_ge(v_read, NT * i + 2 * w + 2)
                else:
                    pe.wait_ge(st_read, NS * i + w - 1)
                for j in range(2):
                    rows = slice(SLOT * j, SLOT * (j + 1))
                    last = nc.tensor.matmul(ring[:, 2 * (w % 2) + j, 0:T - P * kt],
                                            kT[rows, g % 3, pair, P * kt:P * (kt + 1)],
                                            qmT[rows, g % 2, pair, P * kt:T], start=True, stop=True)
                last.then_inc(st_full, 1)

            def weigh(i, n):
                g, kt = divmod(n, NT)
                pe.wait_ge(masked, NG * NT * i + n + 1)
                if n == 0:
                    pe.wait_ge(v_read, NT * (i + 1))
                if kt == 0:
                    wait_if_any(pe, oT_ready, NG * i + g)
                for j in range(HG):
                    last = nc.tensor.matmul(av[32 * j:32 * j + 32, P * kt:T], vs[:, kt, HG * g + j, :],
                                            probs[:, kt, j, P * kt:T], start=kt == 0, stop=kt == NT - 1,
                                            tile_position=(0, 32 * j), skip_group_check=True)
                last.then_inc(av_done, 1)

            def sequence(i, last):
                for w in range(START, NS):
                    s = w + AHEAD
                    if w in V_AT:
                        t = V_AT.index(w)
                        wait_if_any(pe, out_read, NT * (i - 1) + t + 1)
                        project(ring[:, t, :], xT_hi, xT_lo, 2, t, range(NC)).then_inc(v_full, 1)
                    if 0 <= s < NS:
                        score(i, s, 0)
                    if w >= 0:
                        score_transposed(i, w)
                    if 0 <= s < NS:
                        score(i, s, 1)
                    if weighed_at(w) is not None:
                        weigh(i, weighed_at(w))
                    for kind, n in transposes_at(w):
                        transposed(i, kind, n)
                    if not last and 0 <= w - FRONT_AT < FRONT_SLOTS:
                        front(i + 1, w - FRONT_AT)
                for t in range(NT):
                    if t % 2 == 0:
                        pe.wait_ge(st_read, NS * i + NS - 1 + t // 2)
                    if t == 0:
                        pe.wait_ge(turn_read_dve, BY_DVE * (i + 1) - 2)
                    project(ring[:, t, :], aT_hi, aT_lo, 3, t, range(NC - 1))
                    if t in (1, 2):
                        weigh(i, NG * NT - 3 + t)
                if not last:
                    front(i + 1, FRONT_SLOTS)
                transposed(i, "o", NG - 1)
                if not last:
                    front(i + 1, FRONT_SLOTS + 1)
                transposed(i, "a", NC - 1)
                pe.wait_ge(turn_read_dve, BY_DVE * (i + 1))
                for t in range(NT):
                    project(ring[:, t, :], aT_hi, aT_lo, 3, t, range(NC - 1, NC)).then_inc(out_full, 1)

            pe.wait_ge(setup_done, 1)
            pe.wait_ge(consts, 7)
            for f in range(FRONT):
                front(0, f)
            sequence(0, False)
            with pe.Fori(1, NB - 1) as i:
                sequence(i, False)
            sequence(NB - 1, True)


def ffn_phase(nc, x1, gateT, upT, downT, gate_s, up_s, down_s, out):
    ctx = ExitStack()
    with ctx:
        def sb(name, shape, dt=F32):
            return ctx.enter_context(nc.sbuf_tensor(name, shape, dt))

        def pb(name, shape, dt=F32):
            return ctx.enter_context(nc.psum_tensor(name, shape, dt))

        def sem(name):
            return ctx.enter_context(nc.semaphore(name))

        raw = [sb("raw_gate", [P, NC, INTER]), sb("raw_up", [P, NC, INTER]), sb("raw_down", [P, NI, C])]
        gate_hi = sb("gate_hi", [P, NC, INTER], F16)
        gate_lo = sb("gate_lo", [P, NC, INTER], F16)
        up_hi = sb("up_hi", [P, NC, INTER], F16)
        up_lo = sb("up_lo", [P, NC, INTER], F16)
        down_hi = sb("down_hi", [P, NI, C], F16)
        down_lo = sb("down_lo", [P, NI, C], F16)
        ident = sb("f_ident", [P, P])
        neg_half = sb("f_neg_half", [P, NT])
        scales = sb("scales", [P, 3, NI])
        down_row = sb("down_row", [P, C])
        largest = sb("f_largest", [P, 6])
        largest_all = sb("f_largest_all", [P, 6])
        power = sb("f_power", [P, 4])
        scale = sb("f_scale", [P, 4])
        unscale = sb("f_unscale", [P, 4])
        gate_scale = sb("gate_scale", [P, NI])
        up_scale = sb("up_scale", [P, NI])
        rest = sb("rest", [P, 4])
        rest_all = sb("rest_all", [P, 1])
        has_rest = sb("has_rest", [P, 1])

        xn = sb("f_xn", [P, NT, C])
        xr = sb("f_xr", [P, NT, C])
        xT_hi = sb("f_xT_hi", [P, NC, T], F16)
        xT_lo = sb("f_xT_lo", [P, NC, T], F16)
        silu = sb("silu", [P, 2, T])
        hidden = sb("hidden", [P, 2, T])
        hid_hi = sb("hid_hi", [P, 3, T], F16)
        hid_lo = sb("hid_lo", [P, 3, T], F16)
        y = sb("y", [P, NT, C])
        stats = sb("f_stats", [P, NT, 6])
        mv = sb("f_mv", [P, NT, 2])
        var = sb("f_var", [P, NT])
        rstd = sb("f_rstd", [P, NT])
        stats1 = sb("f_stats1", [P, NT, 6])
        mv1 = sb("f_mv1", [P, NT, 2])
        var1 = sb("f_var1", [P, NT])
        rstd1 = sb("f_rstd1", [P, NT])

        gu = pb("gu", [P, 4, 512])
        down = pb("down", [P, NT, 512])

        weights_in = sem("f_weights_in")
        tables_in = sem("f_tables_in")
        consts = sem("f_consts")
        largest_ready = sem("f_largest_ready")
        largest_reduced = sem("f_largest_reduced")
        setup_step = sem("f_setup_step")
        setup_done = sem("f_setup_done")
        x_in = sem("f_x_in")
        xr_in = sem("f_xr_in")
        out_done = sem("out_done")
        var_ready = sem("f_var_ready")
        rstd_ready = sem("f_rstd_ready")
        ln_step = sem("ln_step")
        xn_ready = sem("f_xn_ready")
        xT_full = sem("xT_full")
        hiT_done = sem("f_hiT_done")
        loT_done = sem("loT_done")
        gate_full = sem("gate_full")
        up_full = sem("up_full")
        silu_done = sem("silu_done")
        hidden_done = sem("hidden_done")
        hid_hi_done = sem("hid_hi_done")
        hid_lo_done = sem("hid_lo_done")
        down_step = sem("down_step")
        down_read = sem("down_read")
        var1_ready = sem("f_var1_ready")
        rstd1_ready = sem("f_rstd1_ready")
        end_step = sem("end_step")
        out_ready = sem("out_ready")

        block = ctx.enter_context(nc.Block())

        @block.sync
        def _(sp):
            for r, w in zip(raw, (gateT, upT, downT)):
                sp.dma_start(r[:, :, :], w).then_inc(weights_in, 16)
            sp.dma_start(scales[:, 0, :], gate_s).then_inc(tables_in, 16)
            sp.dma_start(scales[:, 1, :], up_s).then_inc(tables_in, 16)
            sp.dma_start(down_row[:, :], down_s).then_inc(tables_in, 16)
            sp.dma_start(xn[:, :, :], x1[0, :, :, :]).then_inc(x_in, 16)

            def sequence(i, last):
                wait_if_any(sp, out_ready, i)
                if not isinstance(i, int) or i > 0:
                    sp.dma_start(out[i - 1, :, :, :], xr[:, :, :]).then_inc(out_done, 16)
                wait_if_any(sp, out_done, 16 * i)
                sp.dma_start(xr[:, :, :], x1[i, :, :, :]).then_inc(xr_in, 16)
                if not last:
                    sp.wait_ge(xT_full, NC * (i + 1))
                    sp.dma_start(xn[:, :, :], x1[i + 1, :, :, :]).then_inc(x_in, 16)

            sequence(0, False)
            with sp.Fori(1, NB - 1) as i:
                sequence(i, False)
            sequence(NB - 1, True)
            sp.wait_ge(out_ready, NB)
            sp.dma_start(out[NB - 1, :, :, :], xr[:, :, :]).then_inc(out_done, 16)
            sp.wait_ge(out_done, 16 * NB)

        @block.gpsimd
        def _(pool):
            nc.gpsimd.memset(ident[:, :], 0.0).then_inc(consts, 1)
            nc.gpsimd.memset(neg_half[:, :], -0.5).then_inc(consts, 1)
            pool.wait_ge(consts, 2)
            nc.gpsimd.affine_select(out=ident[:, :], in_=ident[:, :], compare_op=ALU.not_equal, fill=1.0, base=0,
                                    pattern=[[-1, P]], channel_multiplier=1).then_inc(consts, 1)
            pool.wait_ge(largest_ready, 1)
            nc.gpsimd.partition_all_reduce(largest_all[:, 0:5], largest[:, 0:5], P, RMAX).then_inc(largest_reduced, 1)
            pool.wait_ge(largest_ready, 2)
            nc.gpsimd.partition_all_reduce(rest_all[:, :], rest[:, 0:1], P, RMAX).then_inc(largest_reduced, 1)

            def inverse_root(i, ready, v, out, done):
                pool.wait_ge(ready, i + 1)
                nc.gpsimd.tensor_tensor(out, v, neg_half[:, :], ALU.pow).then_inc(done, 1)

            inverse_root(0, var_ready, var[:, :], rstd[:, :], rstd_ready)

            inverse_root(1, var_ready, var[:, :], rstd[:, :], rstd_ready)
            with pool.Fori(1, NB - 1) as i:
                inverse_root(i - 1, var1_ready, var1[:, :], rstd1[:, :], rstd1_ready)
                inverse_root(i + 1, var_ready, var[:, :], rstd[:, :], rstd_ready)
            for i in (NB - 2, NB - 1):
                inverse_root(i, var1_ready, var1[:, :], rstd1[:, :], rstd1_ready)

        @block.scalar
        def _(act):
            def sequence(i):
                for c in range(NC):
                    act.wait_ge(xT_full, NC * i + c + 1)
                    nc.scalar.activation(xT_hi[:, c, :], gu[:, c, :], ACT.Copy).then_inc(hiT_done, 1)

                def gate(b):
                    act.wait_ge(gate_full, NI * i + b + 1)
                    wait_if_any(act, hidden_done, NI * i + b - 1)
                    nc.scalar.activation(silu[:, b % 2, :], gu[:, 2 * (b % 2), :], ACT.Silu,
                                         scale=gate_scale[:, b:b + 1]).then_inc(silu_done, 1)

                gate(0)
                for b in range(NI):
                    if b + 1 < NI:
                        gate(b + 1)
                    wait_if_any(act, down_step, NI * i + b - 2)
                    act.wait_ge(hidden_done, NI * i + b + 1)
                    nc.scalar.activation(hid_hi[:, b % 3, :], hidden[:, b % 2, :], ACT.Copy).then_inc(hid_hi_done, 1)

            act.wait_ge(setup_done, 1)
            sequence(0)
            with act.Fori(1, NB) as i:
                sequence(i)

        @block.vector
        def _(dve):
            steps = [0]

            def setup(ins):
                steps[0] += 1
                ins.then_inc(setup_step, 1)
                dve.wait_ge(setup_step, steps[0])

            dve.wait_ge(weights_in, 48)
            dve.wait_ge(tables_in, 48)
            for n in range(3):
                nc.vector.tensor_reduce(largest[:, n:n + 1], raw[n][:, :, :], AX.XY, ALU.max, apply_absolute_value=True)
            nc.vector.tensor_reduce(largest[:, 3:4], scales[:, 0, :], AX.X, ALU.max, apply_absolute_value=True)
            nc.vector.tensor_reduce(largest[:, 4:5], scales[:, 1, :], AX.X, ALU.max,
                                    apply_absolute_value=True).then_inc(largest_ready, 1)
            power_of_two_scales(dve, nc, setup, largest_all[:, 0:3], power[:, 0:3], scale[:, 0:3],
                                unscale[:, 0:3], largest_reduced)
            bound = power[:, 3:4]
            setup(nc.vector.tensor_scalar(bound, largest_all[:, 0:1], largest_all[:, 3:4], float(C), ALU.mult, ALU.mult))
            setup(nc.vector.tensor_scalar(bound, bound, largest_all[:, 1:2], largest_all[:, 4:5], ALU.mult, ALU.mult))
            setup(nc.vector.tensor_scalar(bound, bound, float(C), 2.0 ** -60, ALU.mult, ALU.max))
            setup(nc.vector.tensor_scalar(bound, bound, 2.0 ** 60, None, ALU.min))
            setup(nc.vector.tensor_scalar(bound.bitcast(I32), bound.bitcast(I32), EXPONENT_BITS, None, ALU.bitwise_and))
            setup(nc.vector.reciprocal(scale[:, 3:4], bound))
            setup(nc.vector.tensor_scalar(scale[:, 3:4], scale[:, 3:4], 2.0 ** 14, None, ALU.mult))
            setup(nc.vector.tensor_scalar(unscale[:, 3:4], bound, 2.0 ** -14, None, ALU.mult))
            nc.vector.tensor_scalar(gate_scale[:, :], scales[:, 0, :], unscale[:, 0:1], None, ALU.mult)
            nc.vector.tensor_scalar(up_scale[:, :], scales[:, 1, :], unscale[:, 1:2], scale[:, 3:4], ALU.mult, ALU.mult)
            nc.vector.tensor_scalar(down_row[:, :], down_row[:, :], unscale[:, 2:3], unscale[:, 3:4], ALU.mult, ALU.mult)
            pairs = ((gate_hi, gate_lo), (up_hi, up_lo), (down_hi, down_lo))
            for n, (hi, lo) in enumerate(pairs):
                last = nc.vector.tensor_scalar(hi[:, :, :], raw[n][:, :, :], scale[:, n:n + 1], None, ALU.mult)
            setup(last)
            for n, (hi, lo) in enumerate(pairs):
                last = nc.vector.scalar_tensor_tensor(lo[:, :, :], raw[n][:, :, :], scale[:, n:n + 1], hi[:, :, :],
                                                      ALU.mult, ALU.subtract)
            setup(last)
            for n, (hi, lo) in enumerate(pairs):
                last = nc.vector.tensor_reduce(rest[:, 1 + n:2 + n], lo[:, :, :], AX.XY, ALU.max,
                                               apply_absolute_value=True)
            setup(last)
            nc.vector.tensor_reduce(rest[:, 0:1], rest[:, 1:4], AX.X, ALU.max).then_inc(largest_ready, 1)
            dve.wait_ge(largest_reduced, 2)
            nc.vector.tensor_copy(has_rest[:, :], rest_all[:, :]).then_inc(setup_done, 1)
            dve.wait_ge(setup_done, 1)
            dve.wait_ge(consts, 3)

            def ln2(k):
                def step(ins, stats_next=False):
                    step.n += 1
                    ins.then_inc(ln_step, 1)
                    done = held(dve, 2 * k + step.n)
                    if stats_next:
                        dve.wait_ge(setup_done, 1)
                    dve.wait_ge(ln_step, done)
                step.n = 0
                dve.wait_ge(x_in, 16 * k + 16)
                for t in range(NT):
                    last = nc.vector.bn_stats(stats[:, t, :], xn[:, t, :])
                step(last, True)
                for t in range(NT):
                    last = nc.vector.bn_aggr(mv[:, t, :], stats[:, t, :])
                step(last)
                nc.vector.tensor_scalar(var[:, :], mv[:, :, 1], EPS, None, ALU.add).then_inc(var_ready, 1)
                dve.wait_ge(rstd_ready, k + 1)
                for t in range(NT):
                    last = nc.vector.tensor_scalar(xn[:, t, :], xn[:, t, :], mv[:, t, 0:1], rstd[:, t:t + 1],
                                                   ALU.subtract, ALU.mult)
                last.then_inc(xn_ready, 1)

            def finish(i):
                def step(ins, stats_next=False):
                    step.n += 1
                    ins.then_inc(end_step, 1)
                    done = held(dve, 3 * i + step.n)
                    if stats_next:
                        dve.wait_ge(setup_done, 1)
                    dve.wait_ge(end_step, done)
                step.n = 0
                dve.wait_ge(down_step, NI * (i + 1))
                for t in range(NT):
                    nc.vector.tensor_tensor(y[:, t, :], down[:, t, :], down_row[:, :], ALU.mult).then_inc(down_read, 1)
                for t in range(NT):
                    dve.wait_ge(down_read, NT * i + t + 1)
                    last = nc.vector.bn_stats(stats1[:, t, :], y[:, t, :])
                step(last, True)
                for t in range(NT):
                    last = nc.vector.bn_aggr(mv1[:, t, :], stats1[:, t, :])
                step(last)
                nc.vector.tensor_scalar(var1[:, :], mv1[:, :, 1], EPS, None, ALU.add).then_inc(var1_ready, 1)
                dve.wait_ge(rstd1_ready, i + 1)
                for t in range(NT):
                    last = nc.vector.tensor_scalar(y[:, t, :], y[:, t, :], mv1[:, t, 0:1], rstd1[:, t:t + 1],
                                                   ALU.subtract, ALU.mult)
                step(last)
                dve.wait_ge(xr_in, 16 * i + 16)
                nc.vector.tensor_tensor(xr[:, :, :], xr[:, :, :], y[:, :, :], ALU.add).then_inc(out_ready, 1)

            def sequence(i, last_sequence):
                for c in range(NC):
                    dve.wait_ge(hiT_done, NC * i + c + 1)
                    nc.vector.tensor_tensor(xT_lo[:, c, :], gu[:, c, :], xT_hi[:, c, :], ALU.subtract).then_inc(loT_done, 1)

                def product(b):
                    wait_if_any(dve, hid_hi_done, NI * i + b - 1)
                    wait_if_any(dve, hid_lo_done, NI * i + b - 1)
                    dve.wait_ge(up_full, NI * i + b + 1)
                    dve.wait_ge(silu_done, NI * i + b + 1)
                    nc.vector.scalar_tensor_tensor(hidden[:, b % 2, :], gu[:, 2 * (b % 2) + 1, :], up_scale[:, b:b + 1],
                                                   silu[:, b % 2, :], ALU.mult, ALU.mult).then_inc(hidden_done, 1)

                if not isinstance(i, int) or i > 0:
                    finish(i - 1)
                product(0)
                for b in range(NI):
                    if b + 1 < NI:
                        product(b + 1)
                    wait_if_any(dve, down_step, NI * i + b - 2)
                    dve.wait_ge(hid_hi_done, NI * i + b + 1)
                    nc.vector.tensor_tensor(hid_lo[:, b % 3, :], hidden[:, b % 2, :], hid_hi[:, b % 3, :],
                                            ALU.subtract).then_inc(hid_lo_done, 1)
                    if b == 4 and not last_sequence:
                        ln2(i + 1)

            ln2(0)
            sequence(0, False)
            with dve.Fori(1, NB - 1) as i:
                sequence(i, False)
            sequence(NB - 1, True)
            finish(NB - 1)

        @block.tensor
        def _(pe):
            def sequence(i, with_rest):
                pe.wait_ge(xn_ready, i + 1)
                wait_if_any(pe, hidden_done, NI * i)
                for c in range(NC):
                    for t in range(NT):
                        last = nc.tensor.transpose(gu[:, c, P * t:P * (t + 1)], xn[:, t, P * c:P * (c + 1)], ident[:, :])
                    last.then_inc(xT_full, 1)

                def inner(hi, lo, b, bank):
                    cols = slice(P * b, P * (b + 1))
                    for c in range(NC):
                        nc.tensor.matmul(gu[:, bank, :], hi[:, c, cols], xT_hi[:, c, :], start=c == 0, stop=False)
                        end = c == NC - 1
                        last = nc.tensor.matmul(gu[:, bank, :], hi[:, c, cols], xT_lo[:, c, :], start=False,
                                                stop=end and not with_rest)
                        if with_rest:
                            last = nc.tensor.matmul(gu[:, bank, :], lo[:, c, cols], xT_hi[:, c, :], start=False, stop=end)
                    return last

                def project_down(b):
                    pe.wait_ge(hid_lo_done, NI * i + b + 1)
                    if b == 0:
                        wait_if_any(pe, down_read, NT * i)
                    for t in range(NT):
                        rows = slice(P * t, P * (t + 1))
                        nc.tensor.matmul(down[:, t, :], hid_hi[:, b % 3, rows], down_hi[:, b, :], start=b == 0, stop=False)
                        if with_rest:
                            nc.tensor.matmul(down[:, t, :], hid_hi[:, b % 3, rows], down_lo[:, b, :], start=False,
                                             stop=False)
                        last = nc.tensor.matmul(down[:, t, :], hid_lo[:, b % 3, rows], down_hi[:, b, :], start=False,
                                                stop=b == NI - 1)
                    last.then_inc(down_step, 1)

                pe.wait_ge(loT_done, NC * (i + 1))
                for b in range(NI):
                    wait_if_any(pe, hidden_done, NI * i + b - 1)
                    inner(gate_hi, gate_lo, b, 2 * (b % 2)).then_inc(gate_full, 1)
                    inner(up_hi, up_lo, b, 2 * (b % 2) + 1).then_inc(up_full, 1)
                    if b >= 2:
                        project_down(b - 2)
                project_down(NI - 2)
                project_down(NI - 1)

            pe.wait_ge(setup_done, 1)
            pe.wait_ge(consts, 3)
            any_rest = pe.alloc_register("any_rest")
            pe.reg_load(any_rest, has_rest[0:1, 0:1].bitcast(I32))
            with pe.If_ne(any_rest, 0):
                sequence(0, True)
                with pe.Fori(1, NB) as i:
                    sequence(i, True)
            with pe.Else():
                sequence(0, False)
                with pe.Fori(1, NB) as i:
                    sequence(i, False)


def rope_tables():
    frame, gamma = 144, 0.5
    theta = (np.float32(10000.0) ** (-np.arange(0, DH, 2, dtype=np.float32) / np.float32(DH))).astype(np.float32)
    tok = np.arange(T)
    temporal = np.floor((tok // frame).astype(np.float32) * gamma).astype(np.int32)
    angle = (tok.astype(np.float32)[:, None] * theta).astype(np.float64)
    angle += (temporal.astype(np.float32)[:, None] * theta).astype(np.float64)
    cos = np.concatenate([np.cos(angle), np.cos(angle)], 1).astype(np.float32)
    sin = np.concatenate([-np.sin(angle), np.sin(angle)], 1).astype(np.float32)
    return [np.ascontiguousarray(a.reshape(NT, P, DH).transpose(1, 0, 2)) for a in (cos, sin)]


def by_partition(a, tiles):
    return np.ascontiguousarray(a.reshape(tiles, P, -1).transpose(1, 0, 2))


def kernel(**inputs):
    import concourse.bacc as bacc
    from concourse.bass_utils import run_bass_kernel_spmd

    get = {n.removeprefix("L0_"): np.asarray(a) for n, a in inputs.items()}
    arrays = {"x": np.ascontiguousarray(get["attn_hidden_states"].reshape(NB, NT, P, C).transpose(0, 2, 1, 3))}
    for n in "qkvo":
        arrays[f"w{n}T"] = by_partition(get[f"attn_W{n}"].T, NC)
        arrays[f"b{n}"] = np.ascontiguousarray(np.broadcast_to(get[f"attn_b{n}"], (P, C)))
    arrays["rope_cos"], arrays["rope_sin"] = rope_tables()
    arrays["gateT"] = by_partition(get["ffn_gate_w"].T, NC)
    arrays["upT"] = by_partition(get["ffn_up_w"].T, NC)
    arrays["downT"] = by_partition(get["ffn_down_w"].T, NI)
    arrays["gate_s"] = np.ascontiguousarray(get["ffn_gate_s"].reshape(NI, P).T)
    arrays["up_s"] = np.ascontiguousarray(get["ffn_up_s"].reshape(NI, P).T)
    arrays["down_s"] = np.ascontiguousarray(np.broadcast_to(get["ffn_down_s"], (P, C)))

    nc = bacc.Bacc("TRN2", target_bir_lowering=False, num_devices=1)
    ap = {n: nc.dram_tensor(n, a.shape, mybir.dt.from_np(a.dtype), kind="ExternalInput").ap() for n, a in arrays.items()}
    x1 = nc.dram_tensor("x1", (NB, P, NT, C), F32, kind="Internal").ap()
    out = nc.dram_tensor("out", (NB, P, NT, C), F32, kind="ExternalOutput").ap()
    attention_phase(nc, ap["x"], [ap[f"w{n}T"] for n in "qkvo"], [ap[f"b{n}"] for n in "qkvo"],
                    ap["rope_cos"], ap["rope_sin"], x1)
    ffn_phase(nc, x1, ap["gateT"], ap["upT"], ap["downT"], ap["gate_s"], ap["up_s"], ap["down_s"], out)
    r = run_bass_kernel_spmd(nc, [arrays], core_ids=[0])
    return r.results[0]["out"].transpose(0, 2, 1, 3).reshape(NB, T, C)
```

```python
from contextlib import ExitStack

import numpy as np

import concourse.bass as bass
from concourse import mybir

F32 = mybir.dt.float32
F16 = mybir.dt.float16
I32 = mybir.dt.int32
ALU = mybir.AluOpType
ACT = mybir.ActivationFunctionType
AX = mybir.AxisListType
RMAX = bass.bass_isa.ReduceOp.max

P = 128
NB, T, C = 16, 512, 512
H, DH = 32, 16
NT = T // P
NC = C // P
INTER = 1408
NI = INTER // P
EPS = 1e-5
EXPONENT_BITS = 0x7F800000

HG = 4
NG = H // HG
SLOT = 64
SHIFT_UNIT = 32768.0
NU = 2 * NT


def held(engine, value):
    return value if isinstance(value, int) else engine.to_reg(value)


def wait_if_any(engine, semaphore, value):
    if not isinstance(value, int) or value > 0:
        engine.wait_ge(semaphore, value)


SCALE_STEPS = 4


def power_of_two_scales(dve, nc, link, largest_all, power, scale, unscale, reduced):
    dve.wait_ge(reduced, 1)
    link(nc.vector.tensor_scalar(power, largest_all, 2.0 ** -60, 2.0 ** 60, ALU.max, ALU.min))
    link(nc.vector.tensor_scalar(power.bitcast(I32), power.bitcast(I32), EXPONENT_BITS, None, ALU.bitwise_and))
    link(nc.vector.reciprocal(scale, power))
    link(nc.vector.tensor_scalar(scale, scale, 4.0, None, ALU.mult))
    link(nc.vector.tensor_scalar(unscale, power, 0.25, None, ALU.mult))


def attention_phase(nc, x, wT, bias, rope_cos, rope_sin, x1):
    ctx = ExitStack()
    with ctx:
        def sb(name, shape, dt=F32):
            return ctx.enter_context(nc.sbuf_tensor(name, shape, dt))

        def pb(name, shape, dt=F32):
            return ctx.enter_context(nc.psum_tensor(name, shape, dt))

        def sem(name):
            return ctx.enter_context(nc.semaphore(name))

        w_hi = sb("w_hi", [P, 4, NC, C], F16)
        w_lo = sb("w_lo", [P, 4, NC, C], F16)
        bias_sb = sb("bias_sb", [P, 4, C])
        cos_sb = sb("cos_sb", [P, NT, DH])
        sin_sb = sb("sin_sb", [P, NT, DH])
        ident = sb("ident", [P, P])
        ident16 = sb("ident16", [P, P], F16)
        causal = sb("causal", [P, T])
        neg_half = sb("neg_half", [P, NT])
        largest = sb("largest", [P, 8])
        largest_all = sb("largest_all", [P, 4])
        power = sb("power", [P, 4])
        scale = sb("scale", [P, 4])
        unscale = sb("unscale", [P, 4])
        exp_scale = sb("exp_scale", [P, 1])
        out_unscale = sb("out_unscale", [P, 1])

        xn = sb("xn", [P, NT, C])
        xr = sb("xr", [P, NT, C])
        xT_hi = sb("xT_hi", [P, NC, T], F16)
        xT_lo = sb("xT_lo", [P, NC, T], F16)
        aT_hi = sb("aT_hi", [P, NC, T], F16)
        aT_lo = sb("aT_lo", [P, NC, T], F16)
        qs = sb("qs", [P, NT, H, SLOT], F16)
        ks = sb("ks", [P, NT, H, SLOT], F16)
        vs = sb("vs", [P, NT, H, 32])
        biased = sb("biased", [P, 2, C])
        turned = sb("turned", [P, 2, C])
        roped = sb("roped", [P, 3, C])
        qT = sb("qT", [P, 2, 2, T], F16)
        qmT = sb("qmT", [P, 2, 2, T], F16)
        kTz = [sb(f"kTz{j}", [P, 3, 2, T], F16) for j in range(2)]
        probs = sb("probs", [P, NT, HG, T])
        row_max = sb("row_max", [P, 2, NT, HG])
        shift = sb("shift", [P, NT, HG])
        oT = sb("oT", [P, T])
        recip = sb("recip", [P, NT, HG])
        attn = sb("attn", [P, NT, C])
        stats = sb("stats", [P, NT, 6])
        mv = sb("mv", [P, NT, 2])
        var = sb("var", [P, NT])
        rstd = sb("rstd", [P, NT])
        stats1 = sb("stats1", [P, NT, 6])
        mv1 = sb("mv1", [P, NT, 2])
        var1 = sb("var1", [P, NT])
        rstd1 = sb("rstd1", [P, NT])

        ring = pb("ring", [P, 4, 512])
        narrow = pb("narrow", [P, 2, 512])
        av = pb("av", [P, T])
        turn = pb("turn", [P, T])
        turn16 = turn[:, :].bitcast(F16).rearrange("p (a t) -> p a t", a=2)

        weights_in = [sem(f"weights_in{n}") for n in range(4)]
        padding = sem("padding")
        weights_hi = sem("weights_hi")
        tables_in = sem("tables_in")
        consts = sem("consts")
        largest_ready = sem("largest_ready")
        largest_reduced = sem("largest_reduced")
        setup_step = sem("setup_step")
        setup_done = sem("setup_done")
        x_in = sem("x_in")
        xr_in = sem("xr_in")
        x1_out = sem("x1_out")
        var_ready = sem("var_ready")
        rstd_ready = sem("rstd_ready")
        ln1_step = sem("ln1_step")
        xn_ready = sem("xn_ready")
        narrow_full = sem("narrow_full")
        narrow_free = sem("narrow_free")
        xT_hi_done = sem("xT_hi_done")
        aT_hi_done = sem("aT_hi_done")
        k_and_q_biased = sem("k_and_q_biased")
        turned_done = sem("turned_done")
        roped_done = sem("roped_done")
        qk_hi = sem("qk_hi")
        qk_lo = sem("qk_lo")
        turn_full = sem("turn_full")
        turn_read_act = sem("turn_read_act")
        turn_read_dve = sem("turn_read_dve")
        shift_step = sem("shift_step")
        shift_ready = sem("shift_ready")
        v_full = sem("v_full")
        v_read = sem("v_read")
        st_full = sem("st_full")
        st_read = sem("st_read")
        masked = sem("masked")
        av_done = sem("av_done")
        oT_ready = sem("oT_ready")
        recip_done = sem("recip_done")
        out_full = sem("out_full")
        out_read = sem("out_read")
        out_step = sem("out_step")
        projected_normed = sem("projected_normed")
        var1_ready = sem("var1_ready")
        rstd1_ready = sem("rstd1_ready")
        x1_ready = sem("x1_ready")

        SCALES_AT = 3 + SCALE_STEPS

        NS = NG * NU
        AHEAD = NU + 5
        START = -2 * NU
        FRONT = NC + 2 * NT
        FRONT_AT = NS - AHEAD
        FRONT_SLOTS = NS - FRONT_AT - 2
        N_NARROW = FRONT + 2 * NS
        EARLY = range(NC - 1)
        PARTS_AT = {START: [("out", t, NC - 1) for t in range(3)],
                    START + 1: [("out", 3, c) for c in range(NC // 2)],
                    START + 2: [("out", 3, c) for c in range(NC // 2, NC)]}
        V_PARTS = (1, 1, 1, 1, 2, 2, 2, 1, 1, 1, 2, 1)
        for n in range(NT * NC):
            slot = next(k for k in range(len(V_PARTS)) if n < sum(V_PARTS[:k + 1]))
            PARTS_AT.setdefault(START + 3 + slot, []).append(("v",) + divmod(n, NC))
        STATISTICS_AT = (2 * NU - 1, 3 * NU - 1, 4 * NU - 1, 5 * NU - 1)
        VARIANCE_AT = 5 * NU + 1
        NORMALISE_AT = (FRONT_AT - 4, FRONT_AT - 3, FRONT_AT - 2, FRONT_AT - 1)
        PROJECTED_AT = (-1, 0, 1, 2, 4, 5, 7, 8, 9, 10)
        RESIDUAL_AT = (9, 11, 12, 13)
        A_AT = {3 * NU + 2: 0, 5 * NU + 2: 1, 7 * NU + 2: 2}
        WEIGH_LAG = 6
        QT_OF_UNIT = (2, 2, 3, 3, 1, 1, 0, 0)

        def transposes_at(w):
            g, u = divmod(w, NU)
            out = []
            if w == START:
                out.append(("q", 0))
            if u == 1 and g + 2 < NG:
                out.append(("k", g + 2))
            if w in A_AT:
                out.append(("a", A_AT[w]))
            if u == 3 and g + 3 < NG:
                out.append(("q", g + 3))
            if u == 5 and 0 <= g + 1 < NG:
                out.append(("m", g + 1))
            if u == 7 and g >= 1:
                out.append(("o", g - 1))
            return out

        turn_uses = [use for w in range(START, NS) for use in transposes_at(w)] + [("o", NG - 1), ("a", NC - 1)]
        N_TURN = len(turn_uses)

        def read_by(kinds, use):
            return sum(kind in kinds for kind, _ in turn_uses[:use])

        BY_ACT, BY_DVE = read_by("qmk", N_TURN), read_by("koa", N_TURN)

        def weighed_at(w):
            n = (w - WEIGH_LAG) // 2
            return n if n >= 0 and w % 2 == 0 and n < NG * NT else None

        def unit_of_maximum(s):
            g, u = divmod(s, NU)
            return g, QT_OF_UNIT[u], u % 2

        ST_BANK = (0, 2, 0, 2, 0, 1, 0, 2)
        ST_RELEASED = (2, 2, 2, 2, 2, 3, 2, 4)
        SPARE = 3

        maximum_bank, before, last_use = [], [], {"narrow 0": -2, "narrow 1": -1}
        for h in range(2 * NS):
            w = h // 2 - AHEAD
            g, u = divmod(w - 1, NU)
            spare = ["spare"] if g >= 0 and u >= 4 else []
            bank = min(["narrow 0", "narrow 1"] + spare, key=lambda b: last_use.get(b, -3))
            if bank == "spare" and last_use.get(bank, -3) < 2 * (g * NU + 5 + AHEAD):
                before.append(("st", g * NU + 3))
            else:
                before.append(("s", last_use[bank]))
            maximum_bank.append(bank)
            last_use[bank] = h

        def bank_of_maximum(h):
            return {"narrow 0": narrow[:, 0, :], "narrow 1": narrow[:, 1, :], "spare": ring[:, SPARE, :]}[maximum_bank[h]]

        def spare_used_before(w):
            heads = [h for h in range(2 * max(0, w + AHEAD)) if h < 2 * NS and maximum_bank[h] == "spare"]
            return heads[-1] if heads else None

        def transposed_scores_at(w):
            u = w % NU
            n = T - P * (u // 2)
            if 2 * n <= T:
                return ring[:, ST_BANK[u], 0:2 * n].rearrange("p (j n) -> p j n", j=2)
            return ring[:, ST_BANK[u]:ST_BANK[u] + 2, 0:n]

        block = ctx.enter_context(nc.Block())

        @block.sync
        def _(sp):
            sp.dma_start(xn[:, :, :], x[0, :, :, :]).then_inc(x_in, 16)
            for n in range(4):
                sp.dma_start(probs[:, n, :, :], wT[n]).then_inc(weights_in[n], 16)
            for n in range(4):
                sp.dma_start(bias_sb[:, n, :], bias[n]).then_inc(tables_in, 16)
            sp.dma_start(cos_sb[:, :, :], rope_cos).then_inc(tables_in, 16)
            sp.dma_start(sin_sb[:, :, :], rope_sin).then_inc(tables_in, 16)
            sp.dma_start(xr[:, :, :], x[0, :, :, :]).then_inc(xr_in, 16)

            def sequence(i, last):
                if not last:
                    sp.wait_ge(narrow_full, N_NARROW * i + NC)
                    sp.dma_start(xn[:, :, :], x[i + 1, :, :, :]).then_inc(x_in, 16)
                if not isinstance(i, int) or i > 0:
                    sp.wait_ge(x1_ready, i)
                    sp.dma_start(x1[i - 1, :, :, :], xr[:, :, :]).then_inc(x1_out, 16)
                    sp.wait_ge(x1_out, 16 * i)
                    sp.dma_start(xr[:, :, :], x[i, :, :, :]).then_inc(xr_in, 16)

            sequence(0, False)
            with sp.Fori(1, NB - 1) as i:
                sequence(i, False)
            sequence(NB - 1, True)
            sp.wait_ge(x1_ready, NB)
            sp.dma_start(x1[NB - 1, :, :, :], xr[:, :, :]).then_inc(x1_out, 16)
            sp.wait_ge(x1_out, 16 * NB)

        @block.gpsimd
        def _(pool):
            nc.gpsimd.memset(ident[:, :], 0.0).then_inc(consts, 1)
            nc.gpsimd.memset(ident16[:, :], 0.0).then_inc(consts, 1)
            nc.gpsimd.memset(causal[:, :], 0.0).then_inc(consts, 1)
            nc.gpsimd.memset(neg_half[:, :], -0.5).then_inc(consts, 1)
            pool.wait_ge(consts, 4)
            for m in (ident, ident16):
                nc.gpsimd.affine_select(out=m[:, :], in_=m[:, :], compare_op=ALU.not_equal, fill=1.0, base=0,
                                        pattern=[[-1, P]], channel_multiplier=1).then_inc(consts, 1)
            tri = causal[:, T - P:T]
            nc.gpsimd.affine_select(out=tri, in_=tri, compare_op=ALU.is_ge, fill=-1e38, base=0,
                                    pattern=[[-1, P]], channel_multiplier=1).then_inc(consts, 1)
            def inverse_root(i, ready, v, out, done):
                pool.wait_ge(ready, i + 1)
                nc.gpsimd.tensor_tensor(out, v, neg_half[:, :], ALU.pow).then_inc(done, 1)

            def turn_pairs(i, n):
                t = n % NT
                pool.wait_ge(k_and_q_biased, 2 * NT * i + n + 1)
                a = biased[:, n % 2, :].rearrange("p (h d) -> p h d", h=H)
                o = turned[:, n % 2, :].rearrange("p (h d) -> p h d", h=H)
                s = sin_sb[:, t:t + 1, :]
                half = DH // 2
                nc.gpsimd.tensor_tensor(o[:, :, 0:half], a[:, :, half:DH],
                                        s[:, :, 0:half].broadcast_to([P, H, half]), ALU.mult)
                nc.gpsimd.tensor_tensor(o[:, :, half:DH], a[:, :, 0:half],
                                        s[:, :, half:DH].broadcast_to([P, H, half]), ALU.mult).then_inc(turned_done, 1)

            def mask(i, n):
                kt = n % NT
                exps_done = held(pool, NS * i + 2 * n + 2)
                pool.wait_ge(consts, 7)
                pool.wait_ge(st_read, exps_done)
                d = probs[:, kt, :, P * kt:P * kt + P]
                nc.gpsimd.affine_select(out=d, in_=d, compare_op=ALU.is_ge, fill=0.0, base=0,
                                        pattern=[[0, HG], [1, P]], channel_multiplier=-1).then_inc(masked, 1)

            def residual(i, t):
                if t == 0:
                    pool.wait_ge(xr_in, 16 * (i + 1))
                pool.wait_ge(projected_normed, NT * i + t + 1)
                added = nc.gpsimd.tensor_tensor(xr[:, t, :], xr[:, t, :], attn[:, t, :], ALU.add)
                if t == NT - 1:
                    added.then_inc(x1_ready, 1)

            def sequence(i, last):
                for w in range(2, NS + 1):
                    if w == PROJECTED_AT[NT + 1] + 1 and (not isinstance(i, int) or i > 0):
                        inverse_root(i - 1, var1_ready, var1[:, :], rstd1[:, :], rstd1_ready)
                    if (not isinstance(i, int) or i > 0) and w in RESIDUAL_AT:
                        residual(i - 1, RESIDUAL_AT.index(w))
                    if w % 2 == 0:
                        mask(i, w // 2 - 1)
                    if not last and w == VARIANCE_AT + 3:
                        inverse_root(i + 1, var_ready, var[:, :], rstd[:, :], rstd_ready)
                    n = w - FRONT_AT - NC - 1
                    if not last and 0 <= n < FRONT_SLOTS - NC:
                        turn_pairs(i + 1, n)
                if not last:
                    for n in range(FRONT_SLOTS - NC, 2 * NT):
                        turn_pairs(i + 1, n)

            inverse_root(0, var_ready, var[:, :], rstd[:, :], rstd_ready)
            for operand in (ks, qs, vs):
                nc.gpsimd.memset(operand[:, :, :, :], 0.0).then_inc(padding, 1)
            pool.wait_ge(padding, 3)
            nc.gpsimd.memset(ks[:, :, :, 3 * DH:3 * DH + 2], SHIFT_UNIT).then_inc(padding, 1)
            nc.gpsimd.memset(vs[:, :, :, DH:DH + 1], 1.0).then_inc(padding, 1)
            pool.wait_ge(largest_ready, 1)
            nc.gpsimd.partition_all_reduce(largest_all[:, :], largest[:, 0:4], P, RMAX).then_inc(largest_reduced, 1)
            for n in range(2 * NT):
                turn_pairs(0, n)
            sequence(0, False)
            with pool.Fori(1, NB - 1) as i:
                sequence(i, False)
            sequence(NB - 1, True)
            inverse_root(NB - 1, var1_ready, var1[:, :], rstd1[:, :], rstd1_ready)
            for t in range(NT):
                residual(NB - 1, t)

        @block.scalar
        def _(act):
            def high_of_x(i, c):
                act.wait_ge(narrow_full, N_NARROW * i + c + 1)
                nc.scalar.activation(xT_hi[:, c, :], narrow[:, c % 2, :], ACT.Copy).then_inc(xT_hi_done, 1)

            def high_of_k_or_q(i, n):
                t = n % NT
                act.wait_ge(roped_done, 2 * NT * i + n + 1)
                src = roped[:, n % 3, :].rearrange("p (h o d) -> p h o d", h=H, o=1).broadcast_to([P, H, 2, DH])
                dst = (ks if n < NT else qs)[:, t, :, :].rearrange("p h (s d) -> p h s d", d=DH)
                dst = dst[:, :, 0:2, :] if n < NT else dst[:, :, 0:3:2, :]
                nc.scalar.activation(dst, src, ACT.Copy).then_inc(qk_hi, 1)

            def front(i, f):
                if f < NC:
                    high_of_x(i, f)
                elif f >= NC + 2:
                    high_of_k_or_q(i, f - NC - 2)

            def high_of_attention(i, c):
                act.wait_ge(turn_full, N_TURN * i + turn_uses.index(("a", c)) + 1)
                nc.scalar.activation(aT_hi[:, c, :], turn[:, :], ACT.Copy).then_inc(aT_hi_done, 1)

            def read_transposed(i, kind, g):
                act.wait_ge(turn_full, N_TURN * i + turn_uses.index((kind, g)) + 1)
                if kind == "k":
                    dst, src = kTz[1][SLOT:P, g % 3, :, :], turn16[SLOT:P]
                else:
                    dst, src = (qT if kind == "q" else qmT)[:, g % 2, :, :], turn16
                nc.scalar.activation(dst, src, ACT.Copy).then_inc(turn_read_act, 1)

            def exponentials(i, w):
                g, u = divmod(w, NU)
                kt, pair = divmod(u, 2)
                if g > 0:
                    act.wait_ge(av_done, NG * NT * i + NT * (g - 1) + kt + 1)
                act.wait_ge(st_full, NS * i + w + 1)
                nc.scalar.activation(probs[:, kt, 2 * pair:2 * pair + 2, P * kt:T], transposed_scores_at(w),
                                     ACT.Exp, scale=exp_scale[:, 0:1]).then_inc(st_read, 1)

            def read_weighed(i, g):
                act.wait_ge(av_done, NG * NT * i + NT * (g + 1))
                nc.scalar.activation(oT[:, :], av[:, :], ACT.Copy).then_inc(oT_ready, 1)

            def sequence(i, last):
                for w in range(START, NS):
                    g, u = divmod(w, NU)
                    if u == 5 and g >= 1:
                        read_weighed(i, g - 1)
                    if w >= 0:
                        exponentials(i, w)
                    for kind, n in transposes_at(w):
                        if kind in "qmk":
                            read_transposed(i, kind, n)
                        elif kind == "a":
                            high_of_attention(i, n)
                    if not last and 0 <= w - FRONT_AT < FRONT_SLOTS:
                        front(i + 1, w - FRONT_AT)
                if not last:
                    front(i + 1, FRONT - 1)
                read_weighed(i, NG - 1)
                if not last:
                    front(i + 1, FRONT)
                high_of_attention(i, NC - 1)
                if not last:
                    front(i + 1, FRONT + 1)

            for f in range(NC):
                front(0, f)
            act.wait_ge(setup_step, SCALES_AT)
            for n in (2, 3):
                nc.scalar.activation(w_hi[:, n, :, :], probs[:, n, :, :], ACT.Copy,
                                     scale=scale[:, n:n + 1]).then_inc(weights_hi, 1)
            act.wait_ge(setup_done, 1)
            for f in range(NC, FRONT + 2):
                front(0, f)
            with act.Fori(0, NB - 1) as i:
                sequence(i, False)
            sequence(NB - 1, True)

        @block.vector
        def _(dve):
            steps = [0]

            def setup(ins):
                steps[0] += 1
                ins.then_inc(setup_step, 1)
                dve.wait_ge(setup_step, steps[0])

            def prepare_weights():
                for n in range(4):
                    dve.wait_ge(weights_in[n], 16)
                    nc.vector.tensor_reduce(largest[:, n:n + 1], probs[:, n, :, :], AX.XY, ALU.max,
                                            apply_absolute_value=True)
                dve.wait_ge(tables_in, 96)
                for n in range(4):
                    last = nc.vector.tensor_reduce(largest[:, 4 + n:5 + n], bias_sb[:, n, :], AX.X, ALU.max,
                                                   apply_absolute_value=True)
                setup(last)
                setup(nc.vector.tensor_scalar(largest[:, 4:8], largest[:, 4:8], 1.0 / C, None, ALU.mult))
                nc.vector.tensor_tensor(largest[:, 0:4], largest[:, 0:4], largest[:, 4:8],
                                        ALU.max).then_inc(largest_ready, 1)
                power_of_two_scales(dve, nc, setup, largest_all[:, :], power[:, :], scale[:, :],
                                    unscale[:, :], largest_reduced)
                assert steps[0] > SCALES_AT
                for n in range(3):
                    nc.vector.tensor_scalar(bias_sb[:, n, :], bias_sb[:, n, :], scale[:, n:n + 1], None, ALU.mult)
                nc.vector.tensor_scalar(exp_scale[:, :], unscale[:, 0:1], unscale[:, 1:2], DH ** -0.5,
                                        ALU.mult, ALU.mult)
                nc.vector.tensor_scalar(out_unscale[:, :], unscale[:, 2:3], unscale[:, 3:4], None, ALU.mult)
                for n in range(2):
                    last = nc.vector.tensor_scalar(w_hi[:, n, :, :], probs[:, n, :, :], scale[:, n:n + 1], None,
                                                   ALU.mult)
                setup(last)
                dve.wait_ge(padding, 5)
                for n in range(4):
                    if n >= 2:
                        dve.wait_ge(weights_hi, n - 1)
                    last = nc.vector.scalar_tensor_tensor(w_lo[:, n, :, :], probs[:, n, :, :], scale[:, n:n + 1],
                                                          w_hi[:, n, :, :], ALU.mult, ALU.subtract)
                last.then_inc(setup_done, 1)
                dve.wait_ge(setup_done, 1)

            def await_step(step_semaphore, value, stats_next=False):
                done = held(dve, value)
                if stats_next:
                    dve.wait_ge(consts, 7)
                dve.wait_ge(step_semaphore, done)

            def statistics_of_x(i, t):
                arrived = held(dve, 16 * (i + 1))
                dve.wait_ge(consts, 7)
                dve.wait_ge(x_in, arrived)
                nc.vector.bn_stats(stats[:, t, :], xn[:, t, :]).then_inc(ln1_step, 1)

            def variance_of_x(i):
                await_step(ln1_step, (NT + 1) * i + NT, True)
                for t in range(NT):
                    last = nc.vector.bn_aggr(mv[:, t, :], stats[:, t, :])
                last.then_inc(ln1_step, 1)

            def shifted_variance_of_x(i):
                await_step(ln1_step, (NT + 1) * (i + 1))
                nc.vector.tensor_scalar(var[:, :], mv[:, :, 1], EPS, None, ALU.add).then_inc(var_ready, 1)

            def normalise_x(i, t):
                if t == 0:
                    dve.wait_ge(rstd_ready, i + 1)
                nc.vector.tensor_scalar(xn[:, t, :], xn[:, t, :], mv[:, t, 0:1], rstd[:, t:t + 1],
                                        ALU.subtract, ALU.mult).then_inc(xn_ready, 1)

            def low_of_x(i, c):
                dve.wait_ge(xT_hi_done, NC * i + c + 1)
                nc.vector.tensor_tensor(xT_lo[:, c, :], narrow[:, c % 2, :], xT_hi[:, c, :],
                                        ALU.subtract).then_inc(narrow_free, 1)

            def low_of_attention(i, c):
                dve.wait_ge(aT_hi_done, NC * i + c + 1)
                nc.vector.tensor_tensor(aT_lo[:, c, :], turn[:, :], aT_hi[:, c, :],
                                        ALU.subtract).then_inc(turn_read_dve, 1)

            def bias_and_cosine(i, n):
                t, which = n % NT, 1 - n // NT
                wait_if_any(dve, turned_done, 2 * NT * i + n - 1)
                dve.wait_ge(narrow_full, N_NARROW * i + NC + n + 1)
                nc.vector.tensor_tensor(biased[:, n % 2, :], narrow[:, (NC + n) % 2, :], bias_sb[:, which, :],
                                        ALU.add).then_inc(narrow_free, 1)
                await_step(narrow_free, N_NARROW * i + NC + n + 1)
                r = roped[:, n % 3, :].rearrange("p (h d) -> p h d", h=H)
                nc.vector.tensor_tensor(r, biased[:, n % 2, :].rearrange("p (h d) -> p h d", h=H),
                                        cos_sb[:, t:t + 1, :].broadcast_to([P, H, DH]),
                                        ALU.mult).then_inc(k_and_q_biased, 1)

            def add_sine(i, n):
                dve.wait_ge(turned_done, 2 * NT * i + n + 1)
                nc.vector.tensor_tensor(roped[:, n % 3, :], roped[:, n % 3, :], turned[:, n % 2, :],
                                        ALU.add).then_inc(roped_done, 1)

            def low_of_k_or_q(i, n):
                t = n % NT
                dst, at = (ks, 2 * DH) if n < NT else (qs, DH)
                dve.wait_ge(qk_hi, 2 * NT * i + n + 1)
                nc.vector.tensor_tensor(dst[:, t, :, at:at + DH],
                                        roped[:, n % 3, :].rearrange("p (h d) -> p h d", h=H),
                                        dst[:, t, :, 0:DH], ALU.subtract).then_inc(qk_lo, 1)

            def front(i, f):
                n = f - NC
                if 1 <= f <= NC:
                    low_of_x(i, f - 1)
                if n < 0:
                    return
                if n < 2 * NT:
                    bias_and_cosine(i, n)
                if n >= 2:
                    low_of_k_or_q(i, n - 2)
                if n == NT:
                    nc.vector.memset(qs[:, :, :, 3 * DH:3 * DH + 2], 0.0)
                if 1 <= n <= 2 * NT:
                    add_sine(i, n - 1)

            def bias_v(i, t):
                dve.wait_ge(v_full, NT * i + t + 1)
                nc.vector.tensor_tensor(vs[:, t, :, 0:DH], ring[:, t, :].rearrange("p (h d) -> p h d", h=H),
                                        bias_sb[:, 2, :].rearrange("p (h d) -> p h d", h=H),
                                        ALU.add).then_inc(v_read, 1)

            def read_k(i, g):
                dve.wait_ge(turn_full, N_TURN * i + turn_uses.index(("k", g)) + 1)
                nc.vector.tensor_copy(kTz[0][0:SLOT, g % 3, :, :], turn16[0:SLOT]).then_inc(turn_read_dve, 1)

            def maximum(i, s, j):
                g, qt, pair = unit_of_maximum(s)
                n = P * (qt + 1)
                bank = bank_of_maximum(2 * s + j)
                filled = held(dve, N_NARROW * i + FRONT + 2 * s + j + 1)
                dve.wait_ge(consts, 7)
                dve.wait_ge(narrow_full, filled)
                nc.vector.tensor_tensor_reduce(
                    out=bank[:, 0:n], in0=bank[:, 0:n], in1=causal[:, T - n:T], scale=1.0,
                    scalar=-3e38, op0=ALU.add, op1=ALU.max,
                    accum_out=row_max[:, g % 2, qt, 2 * pair + j:2 * pair + j + 1]).then_inc(narrow_free, 1)

            def maxima_beside_q(i, g, part):
                m = qs[:, :, HG * g:HG * (g + 1), :]
                if part == 0:
                    await_step(narrow_free, N_NARROW * i + FRONT + 2 * NU * (g + 1))
                    nc.vector.tensor_scalar(shift[:, :, :], row_max[:, g % 2, :, :], -1.0 / SHIFT_UNIT, None,
                                            ALU.mult).then_inc(shift_step, 1)
                elif part == 1:
                    await_step(shift_step, 2 * NG * i + 2 * g + 1)
                    nc.vector.tensor_copy(m[:, :, :, 3 * DH], shift[:, :, :]).then_inc(shift_step, 1)
                else:
                    await_step(shift_step, 2 * NG * i + 2 * g + 2)
                    nc.vector.tensor_tensor(m[:, :, :, 3 * DH + 1], shift[:, :, :], m[:, :, :, 3 * DH],
                                            ALU.subtract).then_inc(shift_ready, 1)

            def reciprocal_of_sums(i, g):
                dve.wait_ge(turn_full, N_TURN * i + turn_uses.index(("o", g)) + 1)
                o = turn[:, :].rearrange("p (t h c) -> p t h c", t=NT, c=32)
                nc.vector.reciprocal(recip[:, :, :], o[:, :, :, DH]).then_inc(recip_done, 1)

            def divide_by_sums(i, g):
                if g == 0:
                    wait_if_any(dve, x1_ready, i)
                await_step(recip_done, NG * i + g + 1)
                o = turn[:, :].rearrange("p (t h c) -> p t h c", t=NT, c=32)
                r = recip[:, :, :].rearrange("p t (h o) -> p t h o", o=1).broadcast_to([P, NT, HG, DH])
                dst = attn[:, :, HG * DH * g:HG * DH * (g + 1)].rearrange("p t (h d) -> p t h d", h=HG)
                nc.vector.tensor_tensor(dst, o[:, :, :, 0:DH], r, ALU.mult).then_inc(turn_read_dve, 1)

            def bias_of_projected(i, t):
                dve.wait_ge(out_full, NT * i + t + 1)
                nc.vector.scalar_tensor_tensor(attn[:, t, :], ring[:, t, :], out_unscale[:, 0:1],
                                               bias_sb[:, 3, :], ALU.mult, ALU.add).then_inc(out_read, 1)

            def statistics_of_projected(i, t):
                await_step(out_read, NT * i + t + 1, True)
                nc.vector.bn_stats(stats1[:, t, :], attn[:, t, :]).then_inc(out_step, 1)

            def variance_of_projected(i):
                await_step(out_step, (NT + 1) * i + NT, True)
                for t in range(NT):
                    last = nc.vector.bn_aggr(mv1[:, t, :], stats1[:, t, :])
                last.then_inc(out_step, 1)

            def shifted_variance_of_projected(i):
                await_step(out_step, (NT + 1) * (i + 1))
                nc.vector.tensor_scalar(var1[:, :], mv1[:, :, 1], EPS, None, ALU.add).then_inc(var1_ready, 1)

            def normalise_projected(i, t):
                if t == 0:
                    dve.wait_ge(rstd1_ready, i + 1)
                nc.vector.tensor_scalar(attn[:, t, :], attn[:, t, :], mv1[:, t, 0:1], rstd1[:, t:t + 1],
                                        ALU.subtract, ALU.mult).then_inc(projected_normed, 1)

            def end_of_projection(i, step):
                if step < NT:
                    statistics_of_projected(i, step)
                elif step == NT:
                    variance_of_projected(i)
                elif step == NT + 1:
                    shifted_variance_of_projected(i)
                else:
                    normalise_projected(i, step - NT - 2)

            def sequence(i, last):
                for w in range(START, NS):
                    g, u = divmod(w, NU)
                    s = w + AHEAD
                    if w - 1 in A_AT:
                        low_of_attention(i, A_AT[w - 1])
                    if 0 <= s < NS:
                        maximum(i, s, 0)
                    if s % NU == 0 and 0 < s <= NS:
                        maxima_beside_q(i, s // NU - 1, 0)
                    if s % NU == 1 and 1 < s <= NS + 1:
                        maxima_beside_q(i, s // NU - 1, 2)
                    if u == 0 and g >= 2:
                        reciprocal_of_sums(i, g - 2)
                    for kind, t, c in PARTS_AT.get(w - 1, []):
                        if kind == "v" and c == NC - 1:
                            bias_v(i, t)
                    if 0 <= s < NS:
                        maximum(i, s, 1)
                    if s % NU == 0 and 0 < s <= NS:
                        maxima_beside_q(i, s // NU - 1, 1)
                    if u == 0 and g >= 2:
                        divide_by_sums(i, g - 2)
                    for kind, n in transposes_at(w):
                        if kind == "k":
                            read_k(i, n)
                    if not isinstance(i, int) or i > 0:
                        if w < START + NT:
                            bias_of_projected(i - 1, w - START)
                        if w in PROJECTED_AT:
                            end_of_projection(i - 1, PROJECTED_AT.index(w))
                    if not last:
                        if w in STATISTICS_AT:
                            statistics_of_x(i + 1, STATISTICS_AT.index(w))
                        if w == VARIANCE_AT:
                            variance_of_x(i + 1)
                        if w == VARIANCE_AT + 1:
                            shifted_variance_of_x(i + 1)
                        if w in NORMALISE_AT:
                            normalise_x(i + 1, NORMALISE_AT.index(w))
                        f = w - FRONT_AT
                        if 0 <= f < FRONT_SLOTS:
                            front(i + 1, f)
                reciprocal_of_sums(i, NG - 2)
                divide_by_sums(i, NG - 2)
                if not last:
                    front(i + 1, FRONT - 1)
                reciprocal_of_sums(i, NG - 1)
                divide_by_sums(i, NG - 1)
                if not last:
                    front(i + 1, FRONT)
                low_of_attention(i, NC - 1)
                if not last:
                    front(i + 1, FRONT + 1)

            for zeros in kTz:
                last = nc.vector.memset(zeros[:, :, :, :], 0.0)
            setup(last)
            dve.wait_ge(consts, 7)
            for t in range(NT):
                statistics_of_x(0, t)
            variance_of_x(0)
            shifted_variance_of_x(0)
            for t in range(NT):
                normalise_x(0, t)
            for f in range(NC):
                front(0, f)
            prepare_weights()
            for f in range(NC, FRONT + 2):
                front(0, f)
            sequence(0, False)
            with dve.Fori(1, NB - 1) as i:
                sequence(i, False)
            sequence(NB - 1, True)
            for t in range(NT):
                bias_of_projected(NB - 1, t)
            for step in range(2 * NT + 2):
                end_of_projection(NB - 1, step)

        @block.tensor
        def _(pe):
            def three_products(out, a_hi, a_lo, b_hi, b_lo, first, last):
                nc.tensor.matmul(out, a_hi, b_hi, start=first, stop=False)
                nc.tensor.matmul(out, a_hi, b_lo, start=False, stop=False)
                return nc.tensor.matmul(out, a_lo, b_hi, start=False, stop=last)

            def project(out, hi, lo, w, t, channel_tiles):
                for c in channel_tiles:
                    last = three_products(out, hi[:, c, P * t:P * (t + 1)], lo[:, c, P * t:P * (t + 1)],
                                          w_hi[:, w, c, :], w_lo[:, w, c, :], c == 0, c == NC - 1)
                return last

            def front(i, f):
                if f == 0:
                    pe.wait_ge(xn_ready, NT * (i + 1))
                if f == NC:
                    pe.wait_ge(narrow_free, N_NARROW * i + NC)
                wait_if_any(pe, narrow_free, N_NARROW * i + (f - 1 if f >= 2 else 0))
                bank = narrow[:, f % 2, :]
                if f < NC:
                    for t in range(NT):
                        last = nc.tensor.transpose(bank[:, P * t:P * (t + 1)], xn[:, t, P * f:P * (f + 1)], ident[:, :])
                else:
                    n = f - NC
                    last = project(bank, xT_hi, xT_lo, 1 - n // NT, n % NT, range(NC))
                last.then_inc(narrow_full, 1)

            def transposed(i, kind, n):
                use = turn_uses.index((kind, n))
                if use == 0:
                    wait_if_any(pe, turn_read_dve, BY_DVE * i)
                else:
                    if turn_uses[use - 1][0] in "qmk":
                        pe.wait_ge(turn_read_act, BY_ACT * i + read_by("qmk", use))
                    if turn_uses[use - 1][0] in "koa":
                        pe.wait_ge(turn_read_dve, BY_DVE * i + read_by("koa", use))
                if kind in "qkm":
                    if kind == "m":
                        pe.wait_ge(shift_ready, NG * i + n + 1)
                    elif n == 0:
                        pe.wait_ge(qk_lo, 2 * NT * (i + 1))
                    src = ks if kind == "k" else qs
                    for pair in range(2):
                        for t in range(NT):
                            h = HG * n + 2 * pair
                            last = nc.tensor.transpose(turn16[:, pair, P * t:P * (t + 1)],
                                                       src[:, t, h:h + 2, :].rearrange("p h s -> p (h s)"), ident16[:, :])
                elif kind == "o":
                    pe.wait_ge(oT_ready, NG * i + n + 1)
                    for t in range(NT):
                        last = nc.tensor.transpose(turn[:, P * t:P * (t + 1)], oT[:, P * t:P * (t + 1)], ident[:, :])
                else:
                    pe.wait_ge(turn_read_dve,
                               BY_DVE * i + read_by("koa", turn_uses.index(("o", 2 * n + 1)) + 1))
                    for t in range(NT):
                        last = nc.tensor.transpose(turn[:, P * t:P * (t + 1)], attn[:, t, P * n:P * (n + 1)], ident[:, :])
                last.then_inc(turn_full, 1)

            def score(i, s, j):
                g, qt, pair = unit_of_maximum(s)
                if s % NU == 0 and j == 0:
                    placed = max(turn_uses.index(("q", g)), turn_uses.index(("k", g))) + 1
                    pe.wait_ge(turn_read_act, BY_ACT * i + read_by("qmk", placed))
                    pe.wait_ge(turn_read_dve, BY_DVE * i + read_by("koa", turn_uses.index(("k", g)) + 1))
                kind, use = before[2 * s + j]
                if kind == "st":
                    pe.wait_ge(st_read, NS * i + use + 1)
                else:
                    pe.wait_ge(narrow_free, N_NARROW * i + FRONT + use + 1)
                nc.tensor.matmul(bank_of_maximum(2 * s + j)[:, 0:P * (qt + 1)], qT[:, g % 2, pair, P * qt:P * (qt + 1)],
                                 kTz[j][:, g % 3, pair, 0:P * (qt + 1)], start=True, stop=True).then_inc(narrow_full, 1)

            def score_transposed(i, w):
                g, u = divmod(w, NU)
                kt, pair = divmod(u, 2)
                if u == 0:
                    pe.wait_ge(turn_read_act, BY_ACT * i + read_by("qmk", turn_uses.index(("m", g)) + 1))
                if w < 2:
                    pe.wait_ge(v_read, NT * i + 2 * w + 2)
                else:
                    pe.wait_ge(st_read, NS * i + w - ST_RELEASED[u] + 1)
                    if u == 1 and spare_used_before(w) is not None:
                        pe.wait_ge(narrow_free, N_NARROW * i + FRONT + spare_used_before(w) + 1)
                for j in range(2):
                    last = nc.tensor.matmul(transposed_scores_at(w)[:, j, :],
                                            kTz[j][:, g % 3, pair, P * kt:P * (kt + 1)],
                                            qmT[:, g % 2, pair, P * kt:T], start=True, stop=True)
                last.then_inc(st_full, 1)

            def weigh(i, n):
                g, kt = divmod(n, NT)
                pe.wait_ge(masked, NG * NT * i + n + 1)
                if n == 0:
                    pe.wait_ge(v_read, NT * (i + 1))
                if kt == 0:
                    wait_if_any(pe, oT_ready, NG * i + g)
                for j in range(HG):
                    last = nc.tensor.matmul(av[32 * j:32 * j + 32, P * kt:T], vs[:, kt, HG * g + j, :],
                                            probs[:, kt, j, P * kt:T], start=kt == 0, stop=kt == NT - 1,
                                            tile_position=(0, 32 * j), skip_group_check=True)
                last.then_inc(av_done, 1)

            def project_v(i, t, c):
                if c == 0:
                    wait_if_any(pe, out_read, NT * (i - 1) + t + 1)
                done = project(ring[:, t, :], xT_hi, xT_lo, 2, t, (c,))
                if c == NC - 1:
                    done.then_inc(v_full, 1)

            def project_out(t, channel_tiles):
                done = project(ring[:, t, :], aT_hi, aT_lo, 3, t, channel_tiles)
                if NC - 1 in channel_tiles:
                    done.then_inc(out_full, 1)

            def sequence(i, last):
                for w in range(START, NS):
                    s = w + AHEAD
                    if 0 <= s < NS:
                        score(i, s, 0)
                    if w >= 0:
                        score_transposed(i, w)
                    if 0 <= s < NS:
                        score(i, s, 1)
                    if weighed_at(w) is not None:
                        weigh(i, weighed_at(w))
                    if w == START and (not isinstance(i, int) or i > 0):
                        project_out(2, EARLY)
                    for kind, n in transposes_at(w):
                        transposed(i, kind, n)
                    for kind, t, c in PARTS_AT.get(w, []):
                        if kind == "v":
                            project_v(i, t, c)
                        elif not isinstance(i, int) or i > 0:
                            project_out(t, (c,))
                    if not last and 0 <= w - FRONT_AT < FRONT_SLOTS:
                        front(i + 1, w - FRONT_AT)
                weigh(i, NG * NT - 3)
                if not last:
                    front(i + 1, FRONT - 1)
                weigh(i, NG * NT - 2)
                weigh(i, NG * NT - 1)
                pe.wait_ge(st_read, NS * (i + 1))
                pe.wait_ge(turn_read_dve, BY_DVE * i + read_by("koa", turn_uses.index(("a", NC - 2)) + 1))
                project_out(0, EARLY)
                transposed(i, "o", NG - 1)
                project_out(1, EARLY)
                transposed(i, "a", NC - 1)
                if last:
                    project_out(2, EARLY)
                    pe.wait_ge(turn_read_dve, BY_DVE * (i + 1))
                    for w in range(START, START + 3):
                        for _, t, c in PARTS_AT[w]:
                            project_out(t, (c,))

            pe.wait_ge(consts, 7)
            for f in range(NC):
                front(0, f)
            pe.wait_ge(setup_done, 1)
            for f in range(NC, FRONT):
                front(0, f)
            sequence(0, False)
            with pe.Fori(1, NB - 1) as i:
                sequence(i, False)
            sequence(NB - 1, True)


def ffn_phase(nc, x1, gateT, upT, downT, gate_s, up_s, down_s, out):
    ctx = ExitStack()
    with ctx:
        def sb(name, shape, dt=F32):
            return ctx.enter_context(nc.sbuf_tensor(name, shape, dt))

        def pb(name, shape, dt=F32):
            return ctx.enter_context(nc.psum_tensor(name, shape, dt))

        def sem(name):
            return ctx.enter_context(nc.semaphore(name))

        raw = [sb("raw_gate", [P, NC, INTER]), sb("raw_up", [P, NC, INTER]), sb("raw_down", [P, NI, C])]
        gate_hi = sb("gate_hi", [P, NC, INTER], F16)
        gate_lo = sb("gate_lo", [P, NC, INTER], F16)
        up_hi = sb("up_hi", [P, NC, INTER], F16)
        up_lo = sb("up_lo", [P, NC, INTER], F16)
        down_hi = sb("down_hi", [P, NI, C], F16)
        down_lo = sb("down_lo", [P, NI, C], F16)
        high, low = (gate_hi, up_hi, down_hi), (gate_lo, up_lo, down_lo)
        ident = sb("f_ident", [P, P])
        neg_half = sb("f_neg_half", [P, NT])
        scales = sb("scales", [P, 2, NI])
        down_row = sb("down_row", [P, C])
        largest = sb("f_largest", [P, 5])
        largest_all = sb("f_largest_all", [P, 5])
        power = sb("f_power", [P, 4])
        scale = sb("f_scale", [P, 4])
        unscale = sb("f_unscale", [P, 4])
        gate_scale = sb("gate_scale", [P, NI])
        up_scale = sb("up_scale", [P, NI])
        rest = sb("rest", [P, 3])
        rest_all = sb("rest_all", [P, 3])
        has_rest = sb("has_rest", [P, 1])

        xn = sb("f_xn", [P, NT, C])
        xr = sb("f_xr", [P, NT, C])
        xT_hi = sb("f_xT_hi", [P, NC, T], F16)
        xT_lo = sb("f_xT_lo", [P, NC, T], F16)
        silu = sb("silu", [P, 2, T])
        hidden = sb("hidden", [P, 2, T])
        hid_hi = sb("hid_hi", [P, 3, T], F16)
        hid_lo = sb("hid_lo", [P, 3, T], F16)
        y = sb("y", [P, NT, C])
        stats = sb("f_stats", [P, NT, 6])
        mv = sb("f_mv", [P, NT, 2])
        var = sb("f_var", [P, NT])
        rstd = sb("f_rstd", [P, NT])
        stats1 = sb("f_stats1", [P, NT, 6])
        mv1 = sb("f_mv1", [P, NT, 2])
        var1 = sb("f_var1", [P, NT])
        rstd1 = sb("f_rstd1", [P, NT])

        gu = pb("gu", [P, 4, 512])
        down = pb("down", [P, NT, 512])

        weights_in = [sem(f"f_weights_in{n}") for n in range(3)]
        weights_hi = sem("weights_hi")
        weights_lo = sem("weights_lo")
        rest_ready = sem("rest_ready")
        tables_in = sem("f_tables_in")
        consts = sem("f_consts")
        largest_ready = sem("f_largest_ready")
        largest_reduced = sem("f_largest_reduced")
        setup_step = sem("f_setup_step")
        setup_done = sem("f_setup_done")
        x_in = sem("f_x_in")
        xr_in = sem("f_xr_in")
        out_done = sem("out_done")
        var_ready = sem("f_var_ready")
        rstd_ready = sem("f_rstd_ready")
        ln_step = sem("ln_step")
        xn_ready = sem("f_xn_ready")
        xT_full = sem("xT_full")
        hiT_done = sem("f_hiT_done")
        loT_done = sem("loT_done")
        gate_full = sem("gate_full")
        up_full = sem("up_full")
        silu_done = sem("silu_done")
        hidden_done = sem("hidden_done")
        hid_hi_done = sem("hid_hi_done")
        hid_lo_done = sem("hid_lo_done")
        down_step = sem("down_step")
        down_read = sem("down_read")
        var1_ready = sem("f_var1_ready")
        rstd1_ready = sem("f_rstd1_ready")
        end_step = sem("end_step")
        out_ready = sem("out_ready")

        X_BANK = [(2 * ((NI - 2) % 2) + c) % 4 for c in range(NC)]

        block = ctx.enter_context(nc.Block())

        @block.sync
        def _(sp):
            sp.dma_start(xn[:, :, :], x1[0, :, :, :]).then_inc(x_in, 16)
            sp.dma_start(scales[:, 0, :], gate_s).then_inc(tables_in, 16)
            sp.dma_start(scales[:, 1, :], up_s).then_inc(tables_in, 16)
            sp.dma_start(down_row[:, :], down_s).then_inc(tables_in, 16)
            for n, w in enumerate((gateT, upT, downT)):
                sp.dma_start(raw[n][:, :, :], w).then_inc(weights_in[n], 16)

            def sequence(i, last):
                if not last:
                    sp.wait_ge(xT_full, NC * (i + 1))
                    sp.dma_start(xn[:, :, :], x1[i + 1, :, :, :]).then_inc(x_in, 16)
                wait_if_any(sp, out_ready, i)
                if not isinstance(i, int) or i > 0:
                    sp.dma_start(out[i - 1, :, :, :], xr[:, :, :]).then_inc(out_done, 16)
                wait_if_any(sp, out_done, 16 * i)
                sp.dma_start(xr[:, :, :], x1[i, :, :, :]).then_inc(xr_in, 16)

            sequence(0, False)
            with sp.Fori(1, NB - 1) as i:
                sequence(i, False)
            sequence(NB - 1, True)
            sp.wait_ge(out_ready, NB)
            sp.dma_start(out[NB - 1, :, :, :], xr[:, :, :]).then_inc(out_done, 16)
            sp.wait_ge(out_done, 16 * NB)

        @block.gpsimd
        def _(pool):
            nc.gpsimd.memset(ident[:, :], 0.0).then_inc(consts, 1)
            nc.gpsimd.memset(neg_half[:, :], -0.5).then_inc(consts, 1)
            pool.wait_ge(consts, 2)
            nc.gpsimd.affine_select(out=ident[:, :], in_=ident[:, :], compare_op=ALU.not_equal, fill=1.0, base=0,
                                    pattern=[[-1, P]], channel_multiplier=1).then_inc(consts, 1)
            def inverse_root(i, ready, v, out, done):
                pool.wait_ge(ready, i + 1)
                nc.gpsimd.tensor_tensor(out, v, neg_half[:, :], ALU.pow).then_inc(done, 1)

            inverse_root(0, var_ready, var[:, :], rstd[:, :], rstd_ready)
            pool.wait_ge(largest_ready, 1)
            nc.gpsimd.partition_all_reduce(largest_all[:, 0:5], largest[:, 0:5], P, RMAX).then_inc(largest_reduced, 1)
            pool.wait_ge(rest_ready, 3)
            nc.gpsimd.partition_all_reduce(rest_all[:, :], rest[:, :], P, RMAX).then_inc(largest_reduced, 1)
            inverse_root(1, var_ready, var[:, :], rstd[:, :], rstd_ready)
            with pool.Fori(1, NB - 1) as i:
                inverse_root(i - 1, var1_ready, var1[:, :], rstd1[:, :], rstd1_ready)
                inverse_root(i + 1, var_ready, var[:, :], rstd[:, :], rstd_ready)
            for i in (NB - 2, NB - 1):
                inverse_root(i, var1_ready, var1[:, :], rstd1[:, :], rstd1_ready)

        @block.scalar
        def _(act):
            def high_of_x(i, channel_tiles):
                for c in channel_tiles:
                    act.wait_ge(xT_full, NC * i + c + 1)
                    nc.scalar.activation(xT_hi[:, c, :], gu[:, X_BANK[c], :], ACT.Copy).then_inc(hiT_done, 1)

            def sequence(i, last):
                def gate(b):
                    act.wait_ge(gate_full, NI * i + b + 1)
                    wait_if_any(act, hidden_done, NI * i + b - 1)
                    nc.scalar.activation(silu[:, b % 2, :], gu[:, 2 * (b % 2), :], ACT.Silu,
                                         scale=gate_scale[:, b:b + 1]).then_inc(silu_done, 1)

                gate(0)
                for b in range(NI):
                    if b + 1 < NI:
                        gate(b + 1)
                    wait_if_any(act, down_step, NI * i + b - 2)
                    act.wait_ge(hidden_done, NI * i + b + 1)
                    nc.scalar.activation(hid_hi[:, b % 3, :], hidden[:, b % 2, :], ACT.Copy).then_inc(hid_hi_done, 1)
                    if not last and b >= NI - 2:
                        high_of_x(i + 1, range(2 * (b - NI + 2), 2 * (b - NI + 2) + 2))

            high_of_x(0, range(NC))
            act.wait_ge(setup_step, SCALE_STEPS)
            for n in (1, 2):
                nc.scalar.activation(high[n][:, :, :], raw[n][:, :, :], ACT.Copy,
                                     scale=scale[:, n:n + 1]).then_inc(weights_hi, 1)
            for n in range(3):
                act.wait_ge(weights_lo, n + 1)
                nc.scalar.activation(raw[n][:, :, :], low[n][:, :, :], ACT.Abs,
                                     accum_out=rest[:, n:n + 1]).then_inc(rest_ready, 1)
            act.wait_ge(setup_done, 1)
            sequence(0, False)
            with act.Fori(1, NB - 1) as i:
                sequence(i, False)
            sequence(NB - 1, True)

        @block.vector
        def _(dve):
            steps = [0]

            def setup(ins):
                steps[0] += 1
                ins.then_inc(setup_step, 1)
                dve.wait_ge(setup_step, steps[0])

            def prepare_weights():
                dve.wait_ge(tables_in, 48)
                nc.vector.tensor_reduce(largest[:, 3:4], scales[:, 0, :], AX.X, ALU.max, apply_absolute_value=True)
                nc.vector.tensor_reduce(largest[:, 4:5], scales[:, 1, :], AX.X, ALU.max, apply_absolute_value=True)
                for n in range(3):
                    dve.wait_ge(weights_in[n], 16)
                    last = nc.vector.tensor_reduce(largest[:, n:n + 1], raw[n][:, :, :], AX.XY, ALU.max,
                                                   apply_absolute_value=True)
                last.then_inc(largest_ready, 1)
                power_of_two_scales(dve, nc, setup, largest_all[:, 0:3], power[:, 0:3], scale[:, 0:3],
                                    unscale[:, 0:3], largest_reduced)
                setup(nc.vector.tensor_scalar(high[0][:, :, :], raw[0][:, :, :], scale[:, 0:1], None, ALU.mult))
                for n in range(3):
                    if n > 0:
                        dve.wait_ge(weights_hi, n)
                    nc.vector.scalar_tensor_tensor(low[n][:, :, :], raw[n][:, :, :], scale[:, n:n + 1],
                                                   high[n][:, :, :], ALU.mult, ALU.subtract).then_inc(weights_lo, 1)
                bound = power[:, 3:4]
                setup(nc.vector.tensor_scalar(bound, largest_all[:, 0:1], largest_all[:, 3:4], float(C), ALU.mult, ALU.mult))
                setup(nc.vector.tensor_scalar(bound, bound, largest_all[:, 1:2], largest_all[:, 4:5], ALU.mult, ALU.mult))
                setup(nc.vector.tensor_scalar(bound, bound, float(C), 2.0 ** -60, ALU.mult, ALU.max))
                setup(nc.vector.tensor_scalar(bound, bound, 2.0 ** 60, None, ALU.min))
                setup(nc.vector.tensor_scalar(bound.bitcast(I32), bound.bitcast(I32), EXPONENT_BITS, None, ALU.bitwise_and))
                setup(nc.vector.reciprocal(scale[:, 3:4], bound))
                setup(nc.vector.tensor_scalar(scale[:, 3:4], scale[:, 3:4], 2.0 ** 14, None, ALU.mult))
                setup(nc.vector.tensor_scalar(unscale[:, 3:4], bound, 2.0 ** -14, None, ALU.mult))
                nc.vector.tensor_scalar(gate_scale[:, :], scales[:, 0, :], unscale[:, 0:1], None, ALU.mult)
                nc.vector.tensor_scalar(up_scale[:, :], scales[:, 1, :], unscale[:, 1:2], scale[:, 3:4], ALU.mult, ALU.mult)
                nc.vector.tensor_scalar(down_row[:, :], down_row[:, :], unscale[:, 2:3], unscale[:, 3:4], ALU.mult, ALU.mult)
                dve.wait_ge(largest_reduced, 2)
                nc.vector.tensor_reduce(has_rest[:, :], rest_all[:, :], AX.X, ALU.max).then_inc(setup_done, 1)

            def await_step(step_semaphore, value, stats_next=False):
                done = held(dve, value)
                if stats_next:
                    dve.wait_ge(consts, 3)
                dve.wait_ge(step_semaphore, done)

            def variance_of_x(i):
                dve.wait_ge(x_in, 16 * (i + 1))
                for t in range(NT):
                    last = nc.vector.bn_stats(stats[:, t, :], xn[:, t, :])
                last.then_inc(ln_step, 1)
                await_step(ln_step, 2 * i + 1, True)
                for t in range(NT):
                    last = nc.vector.bn_aggr(mv[:, t, :], stats[:, t, :])
                last.then_inc(ln_step, 1)
                await_step(ln_step, 2 * i + 2)
                nc.vector.tensor_scalar(var[:, :], mv[:, :, 1], EPS, None, ALU.add).then_inc(var_ready, 1)

            def normalise_x(i):
                dve.wait_ge(rstd_ready, i + 1)
                for t in range(NT):
                    last = nc.vector.tensor_scalar(xn[:, t, :], xn[:, t, :], mv[:, t, 0:1], rstd[:, t:t + 1],
                                                   ALU.subtract, ALU.mult)
                last.then_inc(xn_ready, 1)

            def finish(i, part):
                if part == 0:
                    dve.wait_ge(down_step, NI * (i + 1))
                    for t in range(NT):
                        nc.vector.tensor_tensor(y[:, t, :], down[:, t, :], down_row[:, :],
                                                ALU.mult).then_inc(down_read, 1)
                elif part == 1:
                    await_step(down_read, NT * (i + 1), True)
                    for t in range(NT):
                        last = nc.vector.bn_stats(stats1[:, t, :], y[:, t, :])
                    last.then_inc(end_step, 1)
                elif part == 2:
                    await_step(end_step, 3 * i + 1, True)
                    for t in range(NT):
                        last = nc.vector.bn_aggr(mv1[:, t, :], stats1[:, t, :])
                    last.then_inc(end_step, 1)
                    await_step(end_step, 3 * i + 2)
                    nc.vector.tensor_scalar(var1[:, :], mv1[:, :, 1], EPS, None, ALU.add).then_inc(var1_ready, 1)
                elif part == 3:
                    dve.wait_ge(rstd1_ready, i + 1)
                    for t in range(NT):
                        last = nc.vector.tensor_scalar(y[:, t, :], y[:, t, :], mv1[:, t, 0:1], rstd1[:, t:t + 1],
                                                       ALU.subtract, ALU.mult)
                    last.then_inc(end_step, 1)
                else:
                    await_step(end_step, 3 * i + 3)
                    dve.wait_ge(xr_in, 16 * (i + 1))
                    nc.vector.tensor_tensor(xr[:, :, :], xr[:, :, :], y[:, :, :], ALU.add).then_inc(out_ready, 1)

            def low_of_x(i, channel_tiles):
                for c in channel_tiles:
                    dve.wait_ge(hiT_done, NC * i + c + 1)
                    nc.vector.tensor_tensor(xT_lo[:, c, :], gu[:, X_BANK[c], :], xT_hi[:, c, :], ALU.subtract).then_inc(loT_done, 1)

            def sequence(i, last_sequence):
                def product(b):
                    wait_if_any(dve, hid_hi_done, NI * i + b - 1)
                    wait_if_any(dve, hid_lo_done, NI * i + b - 1)
                    dve.wait_ge(up_full, NI * i + b + 1)
                    dve.wait_ge(silu_done, NI * i + b + 1)
                    nc.vector.scalar_tensor_tensor(hidden[:, b % 2, :], gu[:, 2 * (b % 2) + 1, :], up_scale[:, b:b + 1],
                                                   silu[:, b % 2, :], ALU.mult, ALU.mult).then_inc(hidden_done, 1)

                if not isinstance(i, int) or i > 0:
                    finish(i - 1, 0)
                product(0)
                for b in range(NI):
                    if b + 1 < NI:
                        product(b + 1)
                    wait_if_any(dve, down_step, NI * i + b - 2)
                    dve.wait_ge(hid_hi_done, NI * i + b + 1)
                    nc.vector.tensor_tensor(hid_lo[:, b % 3, :], hidden[:, b % 2, :], hid_hi[:, b % 3, :],
                                            ALU.subtract).then_inc(hid_lo_done, 1)
                    if b < 4 and (not isinstance(i, int) or i > 0):
                        finish(i - 1, b + 1)
                    if b == 4 and not last_sequence:
                        variance_of_x(i + 1)
                    if b == 5 and not last_sequence:
                        normalise_x(i + 1)
                    if b >= NI - 2 and not last_sequence:
                        low_of_x(i + 1, range(2 * (b - NI + 2), 2 * (b - NI + 2) + 2))

            variance_of_x(0)
            normalise_x(0)
            low_of_x(0, range(NC))
            prepare_weights()
            sequence(0, False)
            with dve.Fori(1, NB - 1) as i:
                sequence(i, False)
            sequence(NB - 1, True)
            for part in range(5):
                finish(NB - 1, part)

        @block.tensor
        def _(pe):
            def transpose_x(i, channel_tiles):
                if 0 in channel_tiles:
                    pe.wait_ge(xn_ready, i + 1)
                for c in channel_tiles:
                    for t in range(NT):
                        last = nc.tensor.transpose(gu[:, X_BANK[c], P * t:P * (t + 1)], xn[:, t, P * c:P * (c + 1)],
                                                   ident[:, :])
                    last.then_inc(xT_full, 1)

            def sequence(i, with_rest, last_sequence):
                def inner(hi, lo, b, bank):
                    cols = slice(P * b, P * (b + 1))
                    for c in range(NC):
                        nc.tensor.matmul(gu[:, bank, :], hi[:, c, cols], xT_hi[:, c, :], start=c == 0, stop=False)
                        end = c == NC - 1
                        last = nc.tensor.matmul(gu[:, bank, :], hi[:, c, cols], xT_lo[:, c, :], start=False,
                                                stop=end and not with_rest)
                        if with_rest:
                            last = nc.tensor.matmul(gu[:, bank, :], lo[:, c, cols], xT_hi[:, c, :], start=False, stop=end)
                    return last

                def project_down(b):
                    pe.wait_ge(hid_lo_done, NI * i + b + 1)
                    if b == 0:
                        wait_if_any(pe, down_read, NT * i)
                    for t in range(NT):
                        rows = slice(P * t, P * (t + 1))
                        nc.tensor.matmul(down[:, t, :], hid_hi[:, b % 3, rows], down_hi[:, b, :], start=b == 0, stop=False)
                        if with_rest:
                            nc.tensor.matmul(down[:, t, :], hid_hi[:, b % 3, rows], down_lo[:, b, :], start=False,
                                             stop=False)
                        last = nc.tensor.matmul(down[:, t, :], hid_lo[:, b % 3, rows], down_hi[:, b, :], start=False,
                                                stop=b == NI - 1)
                    last.then_inc(down_step, 1)

                pe.wait_ge(loT_done, NC * (i + 1))
                for b in range(NI):
                    wait_if_any(pe, hidden_done, NI * i + b - 1)
                    inner(gate_hi, gate_lo, b, 2 * (b % 2)).then_inc(gate_full, 1)
                    inner(up_hi, up_lo, b, 2 * (b % 2) + 1).then_inc(up_full, 1)
                    if b >= 2:
                        project_down(b - 2)
                for b in (NI - 2, NI - 1):
                    if not last_sequence:
                        pe.wait_ge(hidden_done, NI * i + b + 1)
                        transpose_x(i + 1, range(2 * (b - NI + 2), 2 * (b - NI + 2) + 2))
                    project_down(b)

            pe.wait_ge(consts, 3)
            transpose_x(0, range(NC))
            pe.wait_ge(setup_done, 1)
            any_rest = pe.alloc_register("any_rest")
            pe.reg_load(any_rest, has_rest[0:1, 0:1].bitcast(I32))
            with pe.If_ne(any_rest, 0):
                sequence(0, True, False)
                with pe.Fori(1, NB - 1) as i:
                    sequence(i, True, False)
                sequence(NB - 1, True, True)
            with pe.Else():
                sequence(0, False, False)
                with pe.Fori(1, NB - 1) as i:
                    sequence(i, False, False)
                sequence(NB - 1, False, True)


def rope_tables():
    frame, gamma = 144, 0.5
    theta = (np.float32(10000.0) ** (-np.arange(0, DH, 2, dtype=np.float32) / np.float32(DH))).astype(np.float32)
    tok = np.arange(T)
    temporal = np.floor((tok // frame).astype(np.float32) * gamma).astype(np.int32)
    angle = (tok.astype(np.float32)[:, None] * theta).astype(np.float64)
    angle += (temporal.astype(np.float32)[:, None] * theta).astype(np.float64)
    cos = np.concatenate([np.cos(angle), np.cos(angle)], 1).astype(np.float32)
    sin = np.concatenate([-np.sin(angle), np.sin(angle)], 1).astype(np.float32)
    return [np.ascontiguousarray(a.reshape(NT, P, DH).transpose(1, 0, 2)) for a in (cos, sin)]


def by_partition(a, tiles):
    return np.ascontiguousarray(a.reshape(tiles, P, -1).transpose(1, 0, 2))


def kernel(**inputs):
    import concourse.bacc as bacc
    from concourse.bass_utils import run_bass_kernel_spmd

    get = {n.removeprefix("L0_"): np.asarray(a) for n, a in inputs.items()}
    arrays = {"x": np.ascontiguousarray(get["attn_hidden_states"].reshape(NB, NT, P, C).transpose(0, 2, 1, 3))}
    for n in "qkvo":
        arrays[f"w{n}T"] = by_partition(get[f"attn_W{n}"].T, NC)
        arrays[f"b{n}"] = np.ascontiguousarray(np.broadcast_to(get[f"attn_b{n}"], (P, C)))
    arrays["rope_cos"], arrays["rope_sin"] = rope_tables()
    arrays["gateT"] = by_partition(get["ffn_gate_w"].T, NC)
    arrays["upT"] = by_partition(get["ffn_up_w"].T, NC)
    arrays["downT"] = by_partition(get["ffn_down_w"].T, NI)
    arrays["gate_s"] = np.ascontiguousarray(get["ffn_gate_s"].reshape(NI, P).T)
    arrays["up_s"] = np.ascontiguousarray(get["ffn_up_s"].reshape(NI, P).T)
    arrays["down_s"] = np.ascontiguousarray(np.broadcast_to(get["ffn_down_s"], (P, C)))

    nc = bacc.Bacc("TRN2", target_bir_lowering=False, num_devices=1)
    ap = {n: nc.dram_tensor(n, a.shape, mybir.dt.from_np(a.dtype), kind="ExternalInput").ap() for n, a in arrays.items()}
    x1 = nc.dram_tensor("x1", (NB, P, NT, C), F32, kind="Internal").ap()
    out = nc.dram_tensor("out", (NB, P, NT, C), F32, kind="ExternalOutput").ap()
    attention_phase(nc, ap["x"], [ap[f"w{n}T"] for n in "qkvo"], [ap[f"b{n}"] for n in "qkvo"],
                    ap["rope_cos"], ap["rope_sin"], x1)
    ffn_phase(nc, x1, ap["gateT"], ap["upT"], ap["downT"], ap["gate_s"], ap["up_s"], ap["down_s"], out)
    r = run_bass_kernel_spmd(nc, [arrays], core_ids=[0])
    return r.results[0]["out"].transpose(0, 2, 1, 3).reshape(NB, T, C)
```
